# Optimizing a Trainium2 kernel written in Bass

```python
import numpy as np
import jax
import jax.numpy as jnp

def _softmax(x, axis=-1):
    return jax.nn.softmax(x, axis=axis)

def _gelu(x):
    return jax.nn.gelu(x, approximate=True)

def _silu(x):
    return jax.nn.silu(x)

def _sigmoid(x):
    return jax.nn.sigmoid(x)

def _layernorm(x, axis=-1, eps=1e-05):
    m = jnp.mean(x, axis=axis, keepdims=True)
    v = jnp.var(x, axis=axis, keepdims=True)
    return (x - m) / jnp.sqrt(v + eps)

def _scatter_add(tgt, idx, src, axis=0):
    return tgt.at[idx].add(src)

def _segment_sum(src, seg, n):
    return jax.ops.segment_sum(src, seg, n)
kernel_name = 'mk_macaron_d1_jaxref_r8_f81ab6'

def setup_inputs(seed: int=0):
    np.random.seed(seed)
    _w = jnp.asarray

    def _L0_attn_setup():
        import jax, jax.numpy as jnp
        import numpy as np
        EPS = 1e-05

        def _layer(x, g, b, W_in, b_in, W_h, b_h, W_out, b_out):
            mu = jnp.mean(x, axis=-1, keepdims=True)
            var = jnp.mean(jnp.square(x - mu), axis=-1, keepdims=True)
            x_n = (x - mu) * jax.lax.rsqrt(var + EPS) * g + b
            uv = jnp.einsum('btd,ed->bte', x_n, W_in) + b_in
            d = x.shape[-1]
            u = jnp.transpose(uv[..., :d], (1, 0, 2))
            v = jnp.transpose(uv[..., d:], (1, 0, 2))

            def step(h, uv_t):
                u_t, v_t = uv_t
                gate = jax.nn.sigmoid(u_t)
                cand = jnp.tanh(v_t + h @ W_h.T + b_h)
                h_new = gate * cand + (1.0 - gate) * h
                y = h_new @ W_out.T + b_out
                return (h_new, y)
            h0 = jnp.zeros((x.shape[0], d), dtype=x.dtype)
            _, ys = jax.lax.scan(step, h0, (u, v))
            return x + jnp.transpose(ys, (1, 0, 2))
        key = jax.random.key(seed)
        B, T, D, L = (8, 256, 128, 2)
        ks = jax.random.split(key, 8)
        s = 1.0 / np.sqrt(D)
        return {'x': jax.random.normal(ks[0], (B, T, D), dtype=jnp.float32), 'ln_g': jnp.ones((L, D), dtype=jnp.float32), 'ln_b': jnp.zeros((L, D), dtype=jnp.float32), 'W_in': jax.random.normal(ks[1], (L, 2 * D, D), dtype=jnp.float32) * s, 'b_in': jnp.zeros((L, 2 * D), dtype=jnp.float32), 'W_h': jax.random.normal(ks[2], (L, D, D), dtype=jnp.float32) * s, 'b_h': jnp.zeros((L, D), dtype=jnp.float32), 'W_out': jax.random.normal(ks[3], (L, D, D), dtype=jnp.float32) * s, 'b_out': jnp.zeros((L, D), dtype=jnp.float32)}
    _L0_attn_in = _L0_attn_setup()

    def _L0_ffn_setup():
        import jax, jax.numpy as jnp
        import numpy as np
        TOP_K = 2

        def _ffn(x, gw, uw, dw):
            return jax.nn.silu(x @ gw.T) * (x @ uw.T) @ dw.T
        key = jax.random.key(seed)
        ks = jax.random.split(key, 8)
        w = lambda k, shape: jax.random.normal(k, shape, jnp.float32) * 0.02
        return dict(x=jax.random.normal(ks[0], (4, 256, 128), jnp.float32), gate_w=w(ks[1], (8, 128)), expert_gate=w(ks[2], (8, 352, 128)), expert_up=w(ks[3], (8, 352, 128)), expert_down=w(ks[4], (8, 128, 352)), shared_gate=w(ks[5], (352, 128)), shared_up=w(ks[6], (352, 128)), shared_down=w(ks[7], (128, 352)))
    _L0_ffn_in = _L0_ffn_setup()
    _d = {'L0_attn_x': _L0_attn_in['x'], 'L0_attn_ln_g': _L0_attn_in['ln_g'], 'L0_attn_ln_b': _L0_attn_in['ln_b'], 'L0_attn_W_in': _L0_attn_in['W_in'], 'L0_attn_b_in': _L0_attn_in['b_in'], 'L0_attn_W_h': _L0_attn_in['W_h'], 'L0_attn_b_h': _L0_attn_in['b_h'], 'L0_attn_W_out': _L0_attn_in['W_out'], 'L0_attn_b_out': _L0_attn_in['b_out'], 'L0_ffn_gate_w': _L0_ffn_in['gate_w'], 'L0_ffn_expert_gate': _L0_ffn_in['expert_gate'], 'L0_ffn_expert_up': _L0_ffn_in['expert_up'], 'L0_ffn_expert_down': _L0_ffn_in['expert_down'], 'L0_ffn_shared_gate': _L0_ffn_in['shared_gate'], 'L0_ffn_shared_up': _L0_ffn_in['shared_up'], 'L0_ffn_shared_down': _L0_ffn_in['shared_down']}
    _x0 = _d['L0_attn_x']
    _d['L0_attn_x'] = jax.random.normal(jax.random.fold_in(jax.random.key(seed), 1), (2, 1024, 128), dtype=_x0.dtype)
    del _x0
    return _d

def reference(L0_attn_x, L0_attn_ln_g, L0_attn_ln_b, L0_attn_W_in, L0_attn_b_in, L0_attn_W_h, L0_attn_b_h, L0_attn_W_out, L0_attn_b_out, L0_ffn_gate_w, L0_ffn_expert_gate, L0_ffn_expert_up, L0_ffn_expert_down, L0_ffn_shared_gate, L0_ffn_shared_up, L0_ffn_shared_down):

    def _L0_attn_ref(x, ln_g, ln_b, W_in, b_in, W_h, b_h, W_out, b_out):
        import jax, jax.numpy as jnp
        import numpy as np
        EPS = 1e-05

        def _layer(x, g, b, W_in, b_in, W_h, b_h, W_out, b_out):
            mu = jnp.mean(x, axis=-1, keepdims=True)
            var = jnp.mean(jnp.square(x - mu), axis=-1, keepdims=True)
            x_n = (x - mu) * jax.lax.rsqrt(var + EPS) * g + b
            uv = jnp.einsum('btd,ed->bte', x_n, W_in) + b_in
            d = x.shape[-1]
            u = jnp.transpose(uv[..., :d], (1, 0, 2))
            v = jnp.transpose(uv[..., d:], (1, 0, 2))

            def step(h, uv_t):
                u_t, v_t = uv_t
                gate = jax.nn.sigmoid(u_t)
                cand = jnp.tanh(v_t + h @ W_h.T + b_h)
                h_new = gate * cand + (1.0 - gate) * h
                y = h_new @ W_out.T + b_out
                return (h_new, y)
            h0 = jnp.zeros((x.shape[0], d), dtype=x.dtype)
            _, ys = jax.lax.scan(step, h0, (u, v))
            return x + jnp.transpose(ys, (1, 0, 2))
        out = x
        for l in range(W_in.shape[0]):
            out = _layer(out, ln_g[l], ln_b[l], W_in[l], b_in[l], W_h[l], b_h[l], W_out[l], b_out[l])
        return out

    def _L0_ffn_ref(x, gate_w, expert_gate, expert_up, expert_down, shared_gate, shared_up, shared_down):
        import jax, jax.numpy as jnp
        import numpy as np
        TOP_K = 2

        def _ffn(x, gw, uw, dw):
            return jax.nn.silu(x @ gw.T) * (x @ uw.T) @ dw.T
        B, S, H = x.shape
        xf = x.reshape(-1, H)
        T = xf.shape[0]
        E = expert_gate.shape[0]
        shared = _ffn(xf, shared_gate, shared_up, shared_down)
        logits = xf @ gate_w.T
        probs = jax.nn.softmax(logits, axis=-1)
        topw, topi = jax.lax.top_k(probs, TOP_K)
        topw = topw / (topw.sum(-1, keepdims=True) + 1e-20)
        comb = jnp.zeros((T, E), xf.dtype).at[jnp.arange(T)[:, None], topi].add(topw)

        def body(acc, ws):
            gw, uw, dw, wcol = ws
            return (acc + _ffn(xf, gw, uw, dw) * wcol[:, None], None)
        routed, _ = jax.lax.scan(body, jnp.zeros_like(xf), (expert_gate, expert_up, expert_down, comb.T))
        return (shared + routed).reshape(B, S, H)
    x = L0_attn_x
    x = x + 0.5 * _L0_ffn_ref(_layernorm(x, axis=-1), L0_ffn_gate_w, L0_ffn_expert_gate, L0_ffn_expert_up, L0_ffn_expert_down, L0_ffn_shared_gate, L0_ffn_shared_up, L0_ffn_shared_down)
    x = x + _L0_attn_ref(_layernorm(x, axis=-1), L0_attn_ln_g, L0_attn_ln_b, L0_attn_W_in, L0_attn_b_in, L0_attn_W_h, L0_attn_b_h, L0_attn_W_out, L0_attn_b_out)
    x = x + 0.5 * _L0_ffn_ref(_layernorm(x, axis=-1), L0_ffn_gate_w, L0_ffn_expert_gate, L0_ffn_expert_up, L0_ffn_expert_down, L0_ffn_shared_gate, L0_ffn_shared_up, L0_ffn_shared_down)
    return x

_drawn_inputs = setup_inputs


def setup_inputs(seed=0):
    import zlib

    import numpy as np

    out = dict(_drawn_inputs(seed))
    spreads = {'L0_attn_ln_g': (1.0, 0.2),
     'L0_attn_ln_b': (0.0, 0.1),
     'L0_attn_b_in': (0.0, 0.1),
     'L0_attn_b_h': (0.0, 0.1),
     'L0_attn_b_out': (0.0, 0.1)}
    factors = {'L0_ffn_gate_w': 8.0,
     'L0_ffn_expert_gate': 8.0,
     'L0_ffn_expert_up': 8.0,
     'L0_ffn_expert_down': 8.0,
     'L0_ffn_shared_gate': 8.0,
     'L0_ffn_shared_up': 8.0,
     'L0_ffn_shared_down': 8.0}
    for name, (base, spread) in spreads.items():
        noise = np.random.default_rng([zlib.crc32(name.encode()), seed]).standard_normal(out[name].shape)
        drawn = base * np.exp(spread * noise) if base else spread * noise
        out[name] = jnp.asarray(drawn.astype(out[name].dtype))
    for name, factor in factors.items():
        out[name] = (out[name] * factor).astype(out[name].dtype)
    return out
```

```python
from contextlib import ExitStack

import concourse.bass as bass
from concourse import mybir

F32 = mybir.dt.float32
F16 = mybir.dt.float16
U32 = mybir.dt.uint32
ALU = mybir.AluOpType
ACT = mybir.ActivationFunctionType
AX = mybir.AxisListType

P = 128
STEPS = 64
SEQS = 2
TOK = STEPS * SEQS
LAYERS = 2
EXPERTS = 8
FFNS = 1 + EXPERTS
START = (13, 24)
HALVES = 2 * STEPS
JOB0 = 2
JOB = 4
BASE_P0, BASE_P1, BASE_P2, BASE_FB, BASE_FA = 0, 26, 48, 52, 84
EPS = 1e-5
GUARD = 1e-20
X_SCALE = 16.0
W_SCALE = 64.0
UNSCALE = 1.0 / (X_SCALE * W_SCALE)

IN1 = dict(
    dve=["stats_x", "moments_x", "y", "stats_y", "moments_y", "normed"],
    pool=["eps_x", "rstd_x", "biased", "eps_y", "rstd_y", "gate", "keep", "saved"],
    pe=["turned", "projected"],
    act=["affine", "gate_tanh"])
IN2 = dict(
    dve=["y", "stats_y", "moments_y", "normed"],
    pool=["biased", "eps_y", "rstd_y", "gate", "keep"],
    pe=["read_out", "turned", "projected"],
    act=["affine", "gate_tanh"])
JOIN = dict(dve=["y", "x"], pool=[], pe=["read_out"], act=[])
FFN_IN = dict(
    dve=["stats", "moments", "normed", "low", "top_logit", "total", "inv_total", "top_probs",
         "top_index", "inv_pair"],
    pool=["eps", "rstd", "shifted", "exps", "probs", "pair", "guarded", "weights", "index_f",
          "first", "second", "mix"],
    pe=["turned", "logits"],
    act=["high", "full", "logits_copied"])


class Window:

    def __init__(self, eng, static=None, pair=None, shift=0, products=None,
                 constants=None):
        self.constants = constants
        self.eng, self.static, self.pair, self.shift = eng, static, pair, shift
        self.products = products

    def parity(self, d):
        return (self.static + d) % 2 if self.static is not None else (self.shift + d) % 2

    def tile(self, d):
        return self.static + d if self.static is not None else self.pair * 2 + (self.shift + d)

    def active(self, d, tiles):
        return self.static is None or 0 <= self.static + d < tiles

    def count(self, per, d, c, layer=0):
        if self.static is not None:
            return max(per * (self.static + d) + c, 0)
        if (per, layer) not in self.products:
            self.products[per, layer] = self.pair * (2 * per)
        return self.products[per, layer] + (per * (self.shift + d) + c)

    def apart(self, value):
        if self.static is not None:
            return value
        value = self.eng.to_reg(value)
        self.eng.wait_ge(self.constants, 1)
        return value


class Stage:

    def __init__(self, steps, sems):
        self.steps, self.sem = steps, sems

    def past(self, win, eng, step, d):
        steps = self.steps[eng]
        return win.count(len(steps), d, steps.index(step) + 1)


def macaron(nc, x, ln_g, ln_b, w_in, b_in, b_vh, b_h_row, w_h, w_out, b_out, gate_w, expert_gate,
            expert_up, expert_down, shared_gate, shared_up, shared_down, out):
    T = x.shape[1]
    TILES = T // STEPS
    F = shared_down.shape[0]
    CHUNKS = -(-F // P)
    CH = [min(P, F - c * P) for c in range(CHUNKS)]
    JOBS = FFNS * CHUNKS
    FIRST, LAST = -2, TILES + 2
    LOOP = (4, TILES - 2)

    with ExitStack() as ctx:
        def sb(name, shape, dt=F32):
            return ctx.enter_context(nc.sbuf_tensor(name, shape, dt))

        def sem(name):
            return ctx.enter_context(nc.semaphore(name))

        w32 = [sb(f"w32_{g}", [P, FFNS * F]) for g in range(2)]
        w_hi = [sb(f"w_hi{g}", [P, FFNS * F], F16) for g in range(2)]
        w_lo = [sb(f"w_lo{g}", [P, FFNS * F], F16) for g in range(2)]
        wd = sb("wd", [P, JOBS, P])
        wi = sb("wi", [P, LAYERS, 2 * P])
        wh = sb("wh", [P, LAYERS, P])
        wo = sb("wo", [P, LAYERS, P])
        gw = sb("gw", [P, EXPERTS])
        lng = sb("lng", [P, LAYERS])
        lnb = sb("lnb", [P, LAYERS])
        bu = sb("bu", [P, LAYERS])
        half_bu = sb("half_bu", [P, LAYERS])
        bv_row = sb("bv_row", [P, LAYERS, P])
        bh_row = sb("bh_row", [1, LAYERS, P])
        bo = sb("bo", [P, LAYERS, P])
        ones = sb("ones", [P, TOK])
        ident = sb("ident", [P, P])
        experts = sb("experts", [P, EXPERTS])
        minus_half = sb("minus_half", [P, 1])
        euler = sb("euler", [P, EXPERTS])

        x0 = [sb(f"x0_{q}", [TOK, P]) for q in range(2)]
        acc_a = [sb(f"acc_a{q}", [TOK, P]) for q in range(2)]
        x1 = [sb(f"x1_{q}", [TOK, P]) for q in range(2)]
        x2 = [sb(f"x2_{q}", [TOK, P]) for q in range(2)]
        acc_b = [sb(f"acc_b{q}", [TOK, P]) for q in range(2)]
        xs = [sb(f"xs{q}", [P, 2, 2 * TOK], F16) for q in range(2)]
        comb = {h: [sb(f"comb_{h}{q}", [TOK, EXPERTS]) for q in range(2)] for h in "ab"}
        silu = [sb(f"silu{q}", [P, 2 * TOK]) for q in range(2)]
        hidden = [sb(f"hidden{q}", [P, 2 * TOK]) for q in range(2)]
        y0b = [sb(f"y0b{q}", [TOK, P]) for q in range(2)]
        y1b = [sb(f"y1b{q}", [TOK, P]) for q in range(2)]
        y0 = sb("y0", [TOK, P])
        y1 = sb("y1", [TOK, P])
        y2 = sb("y2", [TOK, P])
        hist = [[sb(f"hist{l}{q}", [P, STEPS, 4]) for q in range(2)] for l in range(LAYERS)]
        gates = [[sb(f"gates{l}{q}", [P, STEPS, 4]) for q in range(2)] for l in range(LAYERS)]
        keeps = [[sb(f"keeps{l}{q}", [P, TOK]) for q in range(2)] for l in range(LAYERS)]
        mixin = [sb(f"mixin{l}", [P, 4]) for l in range(LAYERS)]
        u_tanh = [sb(f"u_tanh{l}", [P, TOK]) for l in range(LAYERS)]
        xn = [sb(f"xn{l}", [TOK, P]) for l in range(LAYERS)]
        xaT = [sb(f"xaT{l}", [P, TOK]) for l in range(LAYERS)]
        st = {s: sb(f"st_{s}", [TOK, 6]) for s in ("x", "y0", "y1", "fa", "fb")}
        mv = {s: sb(f"mv_{s}", [TOK, 2]) for s in ("x", "y0", "y1", "fa", "fb")}
        ve = {s: sb(f"ve_{s}", [TOK, 1]) for s in ("x", "y0", "y1", "fa", "fb")}
        rs = {s: sb(f"rs_{s}", [TOK, 1]) for s in ("x", "y0", "y1", "fa", "fb")}
        fn = {h: sb(f"fn_{h}", [TOK, P]) for h in "ab"}
        fT = {h: sb(f"fT_{h}", [P, TOK]) for h in "ab"}
        rt = {h: {n: sb(f"rt_{n}_{h}", [TOK, w], U32 if n == "index" else F32)
                  for n, w in dict(logits=8, top=8, shifted=8, exps=8, total=1, inv=1, probs=8,
                                   ptop=8, index=8, pair=1, guarded=1, ipair=1, weights=2,
                                   index_f=2, first=8, second=8).items()} for h in "ab"}

        zb = [[ctx.enter_context(nc.psum_tensor(f"zb{l}{q}", [P, 512], F32)) for q in range(2)]
              for l in range(LAYERS)]
        gu = [ctx.enter_context(nc.psum_tensor(f"gu{q}", [P, 2, 2 * TOK], F32)) for q in range(2)]
        dn = [ctx.enter_context(nc.psum_tensor(f"dn{q}", [P, 512], F32)) for q in range(2)]

        w_loaded = sem("w_loaded")
        GROUPS = ((0, 1), (1, 1 + EXPERTS // 2), (1 + EXPERTS // 2, FFNS))
        g_loaded = [sem(f"g_loaded{n}") for n in range(len(GROUPS))]
        d_loaded = [sem(f"d_loaded{n}") for n in range(2)]
        x_loaded = sem("x_loaded")
        out_stored = sem("out_stored")
        consts_dve = sem("consts_dve")
        consts_pool = sem("consts_pool")
        hi_made = sem("hi_made")
        lo_made = sem("lo_made")
        z_ready = [sem(f"z_ready{l}") for l in range(LAYERS)]
        c_ready = [sem(f"c_ready{l}") for l in range(LAYERS)]
        h_ready = [sem(f"h_ready{l}") for l in range(LAYERS)]
        k_ready = [sem(f"k_ready{l}") for l in range(LAYERS)]
        gu_ready = sem("gu_ready")
        silu_ready = sem("silu_ready")
        hid_ready = {h: sem(f"hid_ready_{h}") for h in "ab"}
        dn_ready = sem("dn_ready")
        acc_done = {h: sem(f"acc_done_{h}") for h in "ab"}

        def stage(name, steps):
            return Stage(steps, {e: sem(f"{name}_{e}") for e, s in steps.items() if s})

        in1, in2, join = stage("in1", IN1), stage("in2", IN2), stage("join", JOIN)
        ffn_in = {h: stage(f"ffn_in_{h}", FFN_IN) for h in "ab"}

        block = ctx.enter_context(nc.Block())

        def windows(eng, run):
            for n in range(FIRST, LOOP[0]):
                run(Window(eng, static=n))
            steps2 = eng.alloc_register(f"steps2_{eng.engine.name}")
            eng.reg_mov(steps2, STEPS * LOOP[0])
            with eng.Fori(LOOP[0] // 2, LOOP[1] // 2) as pair:
                products = {(STEPS, 1): eng.snap(steps2)}
                eng.reg_add(steps2, steps2, 2 * STEPS)
                for shift in range(2):
                    run(Window(eng, pair=pair, shift=shift, products=products,
                               constants=consts_dve))
            for n in range(LOOP[1], LAST + 1):
                run(Window(eng, static=n))

        def rnn_step(win, l, slot):
            d = -l if slot >= START[l] else -1 - l
            return (d, (slot - START[l]) % STEPS) if win.active(d, TILES) else None

        def job_at(k, lag):
            j, r = divmod(k - JOB0 - lag, JOB)
            return j if r == 0 and 0 <= j < JOBS else None

        def halves(win):
            return [(h, d) for h, d in (("a", 1), ("b", -3)) if win.active(d, TILES)]

        def span(on):
            return slice(0 if on[0][0] == "a" else TOK, 2 * TOK if on[-1][0] == "b" else TOK)

        def odd(buf):
            return buf[:].rearrange("p t (s z) -> p (t s) z", z=2)[:, :, 1]

        cols = {"a": slice(0, TOK), "b": slice(TOK, 2 * TOK)}
        rows = [slice(e * F + c * P, e * F + c * P + CH[c]) for e in range(FFNS) for c in range(CHUNKS)]

        @block.sync
        def _(sp):
            for dst, src in ((wi, w_in), (wh, w_h), (wo, w_out)):
                sp.dma_start(dst[:], src.rearrange("l d e -> d l e")).then_inc(w_loaded, 16)
            sp.dma_start(gw[:], gate_w).then_inc(w_loaded, 16)
            sp.dma_start(lng[:], ln_g).then_inc(w_loaded, 16)
            sp.dma_start(lnb[:], ln_b).then_inc(w_loaded, 16)
            sp.dma_start(bu[:], b_in).then_inc(w_loaded, 16)
            sp.wait_ge(consts_dve, 1)
            sp.dma_start(bv_row[0:1, :, :], b_vh.rearrange("(a l) d -> a l d", a=1)).then_inc(w_loaded, 16)
            sp.dma_start(bh_row[:], b_h_row.rearrange("(a l) d -> a l d", a=1)).then_inc(w_loaded, 16)
            for l in range(LAYERS):
                sp.dma_start(bo[:, l, :], b_out[l, :].partition_broadcast(P)).then_inc(w_loaded, 16)
            for n, (a, b) in enumerate(GROUPS):
                for g, shared, routed in ((0, shared_gate, expert_gate), (1, shared_up, expert_up)):
                    src = shared if n == 0 else routed[:, (a - 1) * F:(b - 1) * F]
                    sp.dma_start(w32[g][:, a * F:b * F], src).then_inc(g_loaded[n], 16)
            whole = F // P
            wd_v = wd[:].rearrange("p (e c) d -> p e c d", c=CHUNKS)
            sp.dma_start(wd_v[:, 0, 0:whole, :],
                         shared_down[0:whole * P, :].rearrange("(c p) d -> p c d", p=P))\
              .then_inc(d_loaded[0], 16)
            sp.dma_start(wd_v[0:CH[-1], 0, CHUNKS - 1, :], shared_down[F - CH[-1]:F, :])\
              .then_inc(d_loaded[0], 16)
            for c in range(CHUNKS):
                sp.dma_start(wd_v[0:CH[c], 1:FFNS, c, :],
                             expert_down[:, c * P:c * P + CH[c], :].rearrange("e p d -> p e d"))\
                  .then_inc(d_loaded[1], 16)

            def window(win):
                d = 2
                if win.active(d, TILES):
                    sp.wait_ge(acc_done["a"], win.apart(win.count(FFNS, 0, 1)))
                    sp.wait_ge(ffn_in["a"].sem["dve"], win.apart(ffn_in["a"].past(win, "dve", "normed", d - 1)))
                    for s in range(SEQS):
                        t = win.tile(d)
                        src = x[s, bass.ds(t * STEPS, STEPS), :]
                        sp.dma_start(x0[win.parity(d)][s:TOK:SEQS, :], src)\
                          .then_inc(x_loaded, 16)
                d = -3
                if win.active(d, TILES):
                    sp.wait_ge(acc_done["b"], win.apart(win.count(FFNS, d, FFNS)))
                    sp.wait_ge(out_stored, win.apart(win.count(32, d, 0)))
                    for s in range(SEQS):
                        t = win.tile(d)
                        dst = out[s, bass.ds(t * STEPS, STEPS), :]
                        sp.dma_start(dst, acc_b[win.parity(d)][s:TOK:SEQS, :])\
                          .then_inc(out_stored, 16)

            windows(sp, window)
            sp.wait_ge(out_stored, 32 * TILES)

        @block.gpsimd
        def _(pool):
            pool.memset(ident[:], 0.0).then_inc(consts_pool, 1)
            pool.memset(minus_half[:], -0.5).then_inc(consts_pool, 1)
            pool.memset(euler[:], 2.718281828459045).then_inc(consts_pool, 1)
            pool.iota(experts[:], pattern=[[1, EXPERTS]], base=0, channel_multiplier=0,
                      allow_small_or_imprecise_dtypes=True).then_inc(consts_pool, 1)
            pool.wait_ge(consts_pool, 4)
            pool.affine_select(out=ident[:], in_=ident[:], compare_op=ALU.not_equal, fill=1.0,
                               base=0, pattern=[[-1, P]], channel_multiplier=1)\
                .then_inc(consts_pool, 1)
            pool.wait_ge(w_loaded, 16 * 11)
            pool.wait_ge(consts_dve, 4)

            def rstd(win, stg, name, d, moments, suffix=""):
                pool.wait_ge(stg.sem["dve"], win.apart(stg.past(win, "dve", moments, d)))
                pool.tensor_scalar(ve[name][:], mv[name][:, 1:2], EPS, None, ALU.add).then_inc(stg.sem["pool"], 1)
                pool.wait_ge(stg.sem["pool"], win.apart(stg.past(win, "pool", "eps" + suffix, d)))
                pool.tensor_tensor(rs[name][:], ve[name][:], minus_half[:], ALU.pow).then_inc(stg.sem["pool"], 1)

            def gate_and_keep(win, stg, l, d):
                q = win.parity(d)
                pool.wait_ge(stg.sem["act"], win.apart(stg.past(win, "act", "gate_tanh", d)))
                pool.tensor_scalar(odd(gates[l][q]), u_tanh[l][:], 0.5, 0.5, ALU.mult, ALU.add).then_inc(stg.sem["pool"], 1)
                pool.tensor_scalar(keeps[l][q][:], u_tanh[l][:], -0.5, 0.5, ALU.mult, ALU.add).then_inc(stg.sem["pool"], 1)

            def route(win, h, d, q):
                stg, r = ffn_in[h], rt[h]
                pool.wait_ge(stg.sem["dve"], win.apart(stg.past(win, "dve", "top_logit", d)))
                pool.tensor_scalar(r["shifted"][:], r["logits"][:], r["top"][:, 0:1], None,
                                       ALU.subtract).then_inc(stg.sem["pool"], 1)
                pool.wait_ge(stg.sem["pool"], win.apart(stg.past(win, "pool", "shifted", d)))
                pool.tensor_tensor(r["exps"][:], euler[:], r["shifted"][:], ALU.pow).then_inc(stg.sem["pool"], 1)
                pool.wait_ge(stg.sem["dve"], win.apart(stg.past(win, "dve", "inv_total", d)))
                pool.tensor_scalar(r["probs"][:], r["exps"][:], r["inv"][:], None, ALU.mult).then_inc(stg.sem["pool"], 1)
                pool.wait_ge(stg.sem["dve"], win.apart(stg.past(win, "dve", "top_probs", d)))
                pool.tensor_tensor(r["pair"][:], r["ptop"][:, 0:1], r["ptop"][:, 1:2], ALU.add).then_inc(stg.sem["pool"], 1)
                pool.wait_ge(stg.sem["pool"], win.apart(stg.past(win, "pool", "pair", d)))
                pool.tensor_scalar(r["guarded"][:], r["pair"][:], GUARD, None, ALU.add).then_inc(stg.sem["pool"], 1)
                pool.wait_ge(stg.sem["dve"], win.apart(stg.past(win, "dve", "inv_pair", d)))
                pool.tensor_scalar(r["weights"][:], r["ptop"][:, 0:2], r["ipair"][:], 0.5,
                                       ALU.mult, ALU.mult).then_inc(stg.sem["pool"], 1)
                pool.tensor_copy(r["index_f"][:], r["index"][:, 0:2]).then_inc(stg.sem["pool"], 1)
                pool.wait_ge(stg.sem["pool"], win.apart(stg.past(win, "pool", "index_f", d)))
                for n, name in enumerate(("first", "second")):
                    pool.tensor_scalar(r[name][:], experts[:], r["index_f"][:, n:n + 1],
                                           r["weights"][:, n:n + 1], ALU.is_equal, ALU.mult).then_inc(stg.sem["pool"], 1)
                pool.wait_ge(stg.sem["pool"], win.apart(stg.past(win, "pool", "second", d)))
                pool.tensor_tensor(comb[h][q][:], r["first"][:], r["second"][:], ALU.add).then_inc(stg.sem["pool"], 1)

            def window(win):
                d = 0
                if win.active(d, TILES):
                    rstd(win, in1, "x", d, "moments_x", "_x")
                    pool.wait_ge(in1.sem["dve"], win.apart(in1.past(win, "dve", "y", d)))
                    pool.tensor_tensor(y0b[win.parity(d)][:], y0[:], bo[:, 0, :], ALU.add).then_inc(in1.sem["pool"], 1)
                    rstd(win, in1, "y0", d, "moments_y", "_y")
                    gate_and_keep(win, in1, 0, d)
                d = -1
                if win.active(d, TILES):
                    pool.wait_ge(in2.sem["dve"], win.apart(in2.past(win, "dve", "y", d)))
                    pool.tensor_tensor(y1b[win.parity(d)][:], y1[:], bo[:, 1, :], ALU.add).then_inc(in2.sem["pool"], 1)
                    rstd(win, in2, "y1", d, "moments_y", "_y")
                    gate_and_keep(win, in2, 1, d)
                d = 0
                if win.active(d, TILES):
                    pool.wait_ge(join.sem["dve"], win.apart(join.past(win, "dve", "x", d - 2)))
                    pool.tensor_copy(x1[win.parity(d)][:], acc_a[win.parity(d)][:]).then_inc(in1.sem["pool"], 1)
                for h, d in (("b", -2), ("a", 2)):
                    if win.active(d, TILES):
                        rstd(win, ffn_in[h], "f" + h, d, "moments")
                        route(win, h, d, win.parity(1))

            windows(pool, window)

        @block.scalar
        def _(act):
            for e in range(FFNS):
                for n, (a, b) in enumerate(GROUPS):
                    if e == a:
                        act.wait_ge(g_loaded[n], 32)
                for g in range(2):
                    act.activation(w_hi[g][:, e * F:(e + 1) * F], w32[g][:, e * F:(e + 1) * F],
                                   ACT.Copy, scale=W_SCALE).then_inc(hi_made, 1)
            act.wait_ge(consts_dve, 4)

            def drive_in(win, stg, l, k, base, d):
                q = win.parity(d)
                if k == base:
                    act.wait_ge(stg.sem["pe"], stg.past(win, "pe", "turned", d))
                    act.activation(xaT[l][:], zb[l][q][:, 3 * TOK:4 * TOK], ACT.Identity,
                                       scale=lng[:, l:l + 1], bias=lnb[:, l:l + 1]).then_inc(stg.sem["act"], 1)
                if k == base + 4:
                    act.wait_ge(stg.sem["pe"], stg.past(win, "pe", "projected", d))
                    act.activation(u_tanh[l][:], zb[l][q][:, TOK:2 * TOK], ACT.Tanh, scale=0.5,
                                       bias=half_bu[:, l:l + 1]).then_inc(stg.sem["act"], 1)

            def ffn_input(win, h, k, base, d, bank):
                stg = ffn_in[h]
                if k == base + 9:
                    act.wait_ge(stg.sem["pe"], stg.past(win, "pe", "turned", d))
                    act.activation(xs[win.parity(1)][:, 0, cols[h]], bank[:, 3 * TOK:4 * TOK],
                                       ACT.Copy, scale=X_SCALE).then_inc(stg.sem["act"], 1)
                if k == base + 10:
                    act.activation(fT[h][:], bank[:, 3 * TOK:4 * TOK], ACT.Copy).then_inc(stg.sem["act"], 1)
                if k == base + 12:
                    act.wait_ge(stg.sem["pe"], stg.past(win, "pe", "logits", d))
                    act.activation(rt[h]["logits"][:], bank[:, 2 * TOK:2 * TOK + EXPERTS],
                                       ACT.Copy).then_inc(stg.sem["act"], 1)

            def window(win):
                on = halves(win)
                for k in range(HALVES):
                    l = k % 2
                    at = rnn_step(win, l, k // 2)
                    if at:
                        d, t = at
                        act.wait_ge(z_ready[l], win.count(STEPS, d, t + 1, l))
                        z = zb[l][win.parity(d)][:, SEQS * t:SEQS * (t + 1)]
                        act.activation(mixin[l][:, 0:4:2], z, ACT.Tanh).then_inc(c_ready[l], 1)
                    j = job_at(k, 2)
                    if j is not None and on:
                        n, c = CH[j % CHUNKS], span(on)
                        act.wait_ge(gu_ready, win.count(JOBS, 1, j + 1))
                        act.activation(silu[j % 2][0:n, c], gu[j % 2][0:n, 0, c], ACT.Silu,
                                       scale=UNSCALE).then_inc(silu_ready, 1)
                    if win.active(0, TILES):
                        drive_in(win, in1, 0, k, BASE_P0 + 17, 0)
                    if win.active(-1, TILES):
                        drive_in(win, in2, 1, k, BASE_P1 + 12, -1)
                    if win.active(-2, TILES):
                        ffn_input(win, "b", k, BASE_FB, -2, zb[1][win.parity(-2)])
                    if win.active(2, TILES):
                        ffn_input(win, "a", k, BASE_FA, 2, zb[0][win.parity(1)])

            windows(act, window)

        @block.vector
        def _(dve):
            for l in range(LAYERS):
                for q in range(2):
                    dve.memset(gates[l][q][:], 0.0)
                    dve.memset(hist[l][q][:], 0.0)
                dve.memset(mixin[l][:], 0.0)
            dve.memset(bv_row[:], 0.0).then_inc(consts_dve, 1)
            dve.memset(ones[:], 1.0).then_inc(consts_dve, 1)
            dve.wait_ge(w_loaded, 16 * 11)
            dve.tensor_scalar(half_bu[:], bu[:], 0.5, None, ALU.mult).then_inc(consts_dve, 1)
            dve.tensor_tensor(bv_row[0:1, :, :], bv_row[0:1, :, :], bh_row[:], ALU.add)\
               .then_inc(consts_dve, 1)

            def normalise(dst, src, name):
                return dve.tensor_scalar(dst[:], src[:], mv[name][:, 0:1], rs[name][:, 0:1],
                                         ALU.subtract, ALU.mult)

            def in_1(win, k, d):
                if k == BASE_P0:
                    dve.wait_ge(acc_done["a"], win.count(FFNS, d, FFNS))
                    dve.bn_stats(st["x"][:], acc_a[win.parity(d)][:]).then_inc(in1.sem["dve"], 1)
                if k == BASE_P0 + 1:
                    dve.wait_ge(in1.sem["dve"], win.apart(in1.past(win, "dve", "stats_x", d)))
                    dve.bn_aggr(mv["x"][:], st["x"][:]).then_inc(in1.sem["dve"], 1)
                if k == BASE_P0 + 7:
                    dve.wait_ge(in1.sem["pool"], in1.past(win, "pool", "rstd_x", d))
                    normalise(y0, acc_a[win.parity(d)], "x").then_inc(in1.sem["dve"], 1)
                if k == BASE_P0 + 8:
                    dve.wait_ge(in1.sem["dve"], in1.past(win, "dve", "y", d))
                    dve.bn_stats(st["y0"][:], y0[:]).then_inc(in1.sem["dve"], 1)
                if k == BASE_P0 + 9:
                    dve.wait_ge(in1.sem["dve"], win.apart(in1.past(win, "dve", "stats_y", d)))
                    dve.bn_aggr(mv["y0"][:], st["y0"][:]).then_inc(in1.sem["dve"], 1)
                if k == BASE_P0 + 15:
                    dve.wait_ge(in1.sem["pool"], in1.past(win, "pool", "rstd_y", d))
                    normalise(xn[0], y0, "y0").then_inc(in1.sem["dve"], 1)

            def in_2(win, k, d):
                if k == BASE_P1 + 2:
                    dve.wait_ge(in2.sem["pe"], in2.past(win, "pe", "read_out", d))
                    dve.wait_ge(in1.sem["pool"], in1.past(win, "pool", "biased", d))
                    dve.tensor_tensor(y1[:], zb[1][win.parity(d)][:, 2 * TOK:3 * TOK],
                                          y0b[win.parity(d)][:], ALU.add).then_inc(in2.sem["dve"], 1)
                if k == BASE_P1 + 3:
                    dve.wait_ge(in2.sem["dve"], in2.past(win, "dve", "y", d))
                    dve.bn_stats(st["y1"][:], y1[:]).then_inc(in2.sem["dve"], 1)
                if k == BASE_P1 + 4:
                    dve.wait_ge(in2.sem["dve"], win.apart(in2.past(win, "dve", "stats_y", d)))
                    dve.bn_aggr(mv["y1"][:], st["y1"][:]).then_inc(in2.sem["dve"], 1)
                if k == BASE_P1 + 10:
                    dve.wait_ge(in2.sem["pool"], in2.past(win, "pool", "rstd_y", d))
                    normalise(xn[1], y1, "y1").then_inc(in2.sem["dve"], 1)

            def join_x(win, k, d):
                if k == BASE_P2 + 2:
                    dve.wait_ge(join.sem["pe"], join.past(win, "pe", "read_out", d))
                    dve.wait_ge(in2.sem["pool"], in2.past(win, "pool", "biased", d))
                    dve.tensor_tensor(y2[:], zb[1][win.parity(d)][:, 2 * TOK:3 * TOK],
                                          y1b[win.parity(d)][:], ALU.add).then_inc(join.sem["dve"], 1)
                if k == BASE_P2 + 3:
                    dve.wait_ge(join.sem["dve"], join.past(win, "dve", "y", d))
                    dve.wait_ge(in1.sem["pool"], in1.past(win, "pool", "saved", d))
                    dve.tensor_tensor(x2[win.parity(d)][:], y2[:], x1[win.parity(d)][:], ALU.add).then_inc(join.sem["dve"], 1)

            def ffn_input(win, h, k, base, d):
                stg, r, name = ffn_in[h], rt[h], "f" + h
                src = (x0 if h == "a" else x2)[win.parity(d)]
                if k == base:
                    if h == "a":
                        dve.wait_ge(x_loaded, win.count(32, d, 32))
                    else:
                        dve.wait_ge(join.sem["dve"], join.past(win, "dve", "x", d))
                    dve.bn_stats(st[name][:], src[:]).then_inc(stg.sem["dve"], 1)
                if k == base + 1:
                    dve.wait_ge(stg.sem["dve"], win.apart(stg.past(win, "dve", "stats", d)))
                    dve.bn_aggr(mv[name][:], st[name][:]).then_inc(stg.sem["dve"], 1)
                if k == base + 7:
                    dve.wait_ge(stg.sem["pool"], stg.past(win, "pool", "rstd", d))
                    normalise(fn[h], src, name).then_inc(stg.sem["dve"], 1)
                if k == base + 12:
                    dve.wait_ge(stg.sem["act"], stg.past(win, "act", "full", d))
                    dve.scalar_tensor_tensor(
                        out=xs[win.parity(1)][:, 1, cols[h]], in0=fT[h][:], scalar=X_SCALE,
                        in1=xs[win.parity(1)][:, 0, cols[h]], op0=ALU.mult, op1=ALU.subtract).then_inc(stg.sem["dve"], 1)
                if k == base + 14:
                    dve.wait_ge(stg.sem["act"], win.apart(stg.past(win, "act", "logits_copied", d)))
                    dve.max(r["top"][:], r["logits"][:]).then_inc(stg.sem["dve"], 1)
                if k == base + 21:
                    dve.wait_ge(stg.sem["pool"], stg.past(win, "pool", "exps", d))
                    dve.tensor_reduce(r["total"][:], r["exps"][:], AX.X, ALU.add).then_inc(stg.sem["dve"], 1)
                if k == base + 22:
                    dve.wait_ge(stg.sem["dve"], stg.past(win, "dve", "total", d))
                    dve.reciprocal(r["inv"][:], r["total"][:]).then_inc(stg.sem["dve"], 1)
                if k == base + 24:
                    dve.wait_ge(stg.sem["pool"], win.apart(stg.past(win, "pool", "probs", d)))
                    dve.max(r["ptop"][:], r["probs"][:]).then_inc(stg.sem["dve"], 1)
                if k == base + 25:
                    dve.wait_ge(stg.sem["dve"], win.apart(stg.past(win, "dve", "top_probs", d)))
                    dve.max_index(r["index"][:], r["ptop"][:], r["probs"][:]).then_inc(stg.sem["dve"], 1)
                if k == base + 28:
                    dve.wait_ge(stg.sem["pool"], stg.past(win, "pool", "guarded", d))
                    dve.reciprocal(r["ipair"][:], r["guarded"][:]).then_inc(stg.sem["dve"], 1)

            def split_low(e):
                for g in range(2):
                    dve.wait_ge(hi_made, 2 * e + g + 1)
                    part = slice(e * F, (e + 1) * F)
                    dve.scalar_tensor_tensor(out=w_lo[g][:, part], in0=w32[g][:, part],
                                             scalar=W_SCALE, in1=w_hi[g][:, part], op0=ALU.mult,
                                             op1=ALU.subtract).then_inc(lo_made, 1)

            for e in range(FFNS):
                split_low(e)

            def multiply(win, h, d, j):
                n, c = CH[j % CHUNKS], cols[h]
                dve.wait_ge(silu_ready, win.count(JOBS, 1, j + 1))
                dve.scalar_tensor_tensor(out=hidden[j % 2][0:n, c], in0=gu[j % 2][0:n, 1, c],
                                         scalar=UNSCALE, in1=silu[j % 2][0:n, c], op0=ALU.mult,
                                         op1=ALU.mult).then_inc(hid_ready[h], 1)

            def accumulate(win, h, d, e):
                src = dn[win.parity(e)][:, cols[h]]
                acc = (acc_a if h == "a" else acc_b)[win.parity(d)]
                dve.wait_ge(dn_ready, win.count(FFNS, 1, e + 1))
                if e == 0:
                    if h == "a":
                        dve.wait_ge(in1.sem["pool"], in1.past(win, "pool", "saved", d - 2))
                    else:
                        dve.wait_ge(out_stored, win.count(32, d, 0))
                    ins = dve.scalar_tensor_tensor(
                        out=acc[:], in0=src, scalar=0.5, in1=(x0 if h == "a" else x2)[win.parity(d)][:],
                        op0=ALU.mult, op1=ALU.add)
                else:
                    dve.wait_ge(acc_done[h], win.count(FFNS, d, e))
                    if e == 1:
                        dve.wait_ge(ffn_in[h].sem["pool"], ffn_in[h].past(win, "pool", "mix", d))
                    ins = dve.scalar_tensor_tensor(
                        out=acc[:], in0=src, scalar=comb[h][win.parity(0)][:, e - 1:e], in1=acc[:],
                        op0=ALU.mult, op1=ALU.add)
                ins.then_inc(acc_done[h], 1)

            def window(win):
                on = halves(win)
                for k in range(HALVES):
                    l = k % 2
                    at = rnn_step(win, l, k // 2)
                    if at:
                        d, t = at
                        q = win.parity(d)
                        dve.wait_ge(c_ready[l], win.count(STEPS, d, t + 1, l))
                        if win.static is not None and win.static + d == 0 and t == 0:
                            dve.wait_ge((in1, in2)[l].sem["pool"], (in1, in2)[l].past(win, "pool", "keep", d))
                        dve.wait_ge(k_ready[l], win.count(STEPS, d, t, l))
                        dve.tensor_tensor_scan(out=hist[l][q][:, t, :], data0=gates[l][q][:, t, :],
                                               data1=mixin[l][:], initial=0.0, op0=ALU.mult,
                                               op1=ALU.add).then_inc(h_ready[l], 1)
                        nd, nt = (d, t + 1) if t + 1 < STEPS else (d + 1, 0)
                        if win.active(nd, TILES):
                            if nt == 0:
                                dve.wait_ge((in1, in2)[l].sem["pool"], (in1, in2)[l].past(win, "pool", "keep", nd))
                            dve.wait_ge(h_ready[l], win.count(STEPS, d, t + 1, l))
                            dve.tensor_tensor(mixin[l][:, 1:4:2], hist[l][q][:, t, 1:4:2],
                                              keeps[l][win.parity(nd)][:, SEQS * nt:SEQS * (nt + 1)], ALU.mult)\
                               .then_inc(k_ready[l], 1)
                    for h, lag in (("a", 3), ("b", 4)):
                        j = job_at(k, lag)
                        if j is not None:
                            for hh, d in on:
                                if hh == h:
                                    multiply(win, h, d, j)
                    for h, lag in (("a", 2 * JOB + 1), ("b", 2 * JOB + 2)):
                        j = job_at(k, lag)
                        if j is not None and j % CHUNKS == CHUNKS - 1:
                            for hh, d in on:
                                if hh == h:
                                    accumulate(win, h, d, j // CHUNKS)
                    if win.active(0, TILES):
                        in_1(win, k, 0)
                    if win.active(-1, TILES):
                        in_2(win, k, -1)
                    if win.active(-2, TILES):
                        join_x(win, k, -2)
                        ffn_input(win, "b", k, BASE_FB, -2)
                    if win.active(2, TILES):
                        ffn_input(win, "a", k, BASE_FA, 2)

            windows(dve, window)

        @block.tensor
        def _(pe):
            pe.wait_ge(w_loaded, 16 * 11)
            pe.wait_ge(consts_dve, 4)
            pe.wait_ge(consts_pool, 5)

            def project(win, stg, l, k, base, d):
                bank = zb[l][win.parity(d)]
                if k == base:
                    if l == 0 and win.active(d + 1, TILES):
                        pe.wait_ge(ffn_in["a"].sem["act"], ffn_in["a"].past(win, "act", "logits_copied", d + 1))
                    pe.wait_ge(stg.sem["dve"], stg.past(win, "dve", "normed", d))
                    pe.transpose(bank[:, 3 * TOK:4 * TOK], xn[l][:], ident[:]).then_inc(stg.sem["pe"], 1)
                if k == base + 2:
                    pe.wait_ge(stg.sem["act"], stg.past(win, "act", "affine", d))
                    pe.matmul(bank[:, 0:TOK], wi[:, l, P:2 * P], xaT[l][:], start=True, stop=False,
                              skip_group_check=True)
                    pe.matmul(bank[:, 0:TOK], bv_row[:, l, :], ones[:], start=False, stop=False,
                              skip_group_check=True)
                    pe.matmul(bank[:, TOK:2 * TOK], wi[:, l, 0:P], xaT[l][:], start=False, stop=True,
                                  skip_group_check=True).then_inc(stg.sem["pe"], 1)

            def read_out(win, stg, l, k, base, d):
                if k == base:
                    q = win.parity(d)
                    if l == 0:
                        pe.wait_ge(ffn_in["b"].sem["act"], ffn_in["b"].past(win, "act", "logits_copied", d - 2))
                    pe.wait_ge(h_ready[l], win.count(STEPS, d, STEPS, l))
                    pe.matmul(zb[1][q][:, 2 * TOK:3 * TOK], odd(hist[l][q]), wo[:, l, :], start=True, stop=True,
                                  skip_group_check=True).then_inc(stg.sem["pe"], 1)

            def ffn_input(win, h, k, base, d, bank):
                stg = ffn_in[h]
                if k == base + 8:
                    pe.wait_ge(stg.sem["dve"], stg.past(win, "dve", "normed", d))
                    pe.transpose(bank[:, 3 * TOK:4 * TOK], fn[h][:], ident[:]).then_inc(stg.sem["pe"], 1)
                if k == base + 11:
                    pe.wait_ge(stg.sem["act"], stg.past(win, "act", "full", d))
                    pe.matmul(bank[:, 2 * TOK:2 * TOK + EXPERTS], fT[h][:], gw[:], start=True,
                                  stop=True, skip_group_check=True).then_inc(stg.sem["pe"], 1)

            def gate_or_up(win, on, j, g):
                e, ch = divmod(j, CHUNKS)
                n, c, q = CH[ch], span(on), j % 2
                src = xs[win.parity(0)]
                if g == 0:
                    for h, d in (("a", 1), ("b", -3)):
                        if win.active(d, TILES) or (j < 2 and win.static + d == TILES):
                            pe.wait_ge(hid_ready[h], win.count(JOBS, d, max(j - 1, 0)))
                    if j == 0:
                        for h, d in on:
                            pe.wait_ge(ffn_in[h].sem["dve"], ffn_in[h].past(win, "dve", "low", d))
                    if win.static == -1:
                        pe.wait_ge(lo_made, 2 * e + 2)
                dst = gu[q][0:n, g, c]
                r = rows[j]
                pe.matmul(dst, w_hi[g][:, r], src[:, 0, c], start=(g == 0), stop=False,
                          skip_group_check=True)
                pe.matmul(dst, w_hi[g][:, r], src[:, 1, c], start=False, stop=False,
                          skip_group_check=True)
                last = pe.matmul(dst, w_lo[g][:, r], src[:, 0, c], start=False, stop=True,
                                 skip_group_check=True)
                if g == 1:
                    last.then_inc(gu_ready, 1)

            def down(win, on, j, h):
                e, ch = divmod(j, CHUNKS)
                n, first, last = CH[ch], on[0][0], on[-1][0]
                if h == first and ch == 0:
                    if win.static == -1 and e < 2:
                        pe.wait_ge(d_loaded[e], 16 * (2 if e == 0 else CHUNKS))
                    for hh, d in (("a", 1), ("b", -3)):
                        if win.active(d, TILES) or (e < 2 and win.static + d == TILES):
                            pe.wait_ge(acc_done[hh], win.count(FFNS, d, e - 1))
                for hh, d in on:
                    if hh == h:
                        pe.wait_ge(hid_ready[h], win.count(JOBS, d, j + 1))
                        mm = pe.matmul(dn[win.parity(e)][:, cols[h]], hidden[j % 2][0:n, cols[h]],
                                       wd[0:n, j, :], start=(ch == 0 and h == first),
                                       stop=(ch == CHUNKS - 1), skip_group_check=True)
                        if ch == CHUNKS - 1 and h == last:
                            mm.then_inc(dn_ready, 1)

            def window(win):
                on = halves(win)
                for k in range(HALVES):
                    l = k % 2
                    at = rnn_step(win, l, k // 2)
                    if at:
                        d, t = at
                        pd, pt = (d, t - 1) if t else (d - 1, STEPS - 1)
                        if t == 0:
                            pe.wait_ge((in1, in2)[l].sem["act"], (in1, in2)[l].past(win, "act", "gate_tanh", d))
                        pe.wait_ge(h_ready[l], win.count(STEPS, d, t, l))
                        z = zb[l][win.parity(d)][:, SEQS * t:SEQS * (t + 1)]
                        pe.matmul(z, wh[:, l, :], hist[l][win.parity(pd)][:, pt, 1:4:2], start=False,
                                  stop=True, skip_group_check=True).then_inc(z_ready[l], 1)
                    if on:
                        j = job_at(k, 0)
                        if j is not None:
                            gate_or_up(win, on, j, 0)
                        j = job_at(k, 1)
                        if j is not None:
                            gate_or_up(win, on, j, 1)
                        for h, lag in (("a", JOB + 2), ("b", JOB + 3)):
                            j = job_at(k, lag)
                            if j is not None:
                                down(win, on, j, h)
                    if win.active(0, TILES):
                        project(win, in1, 0, k, BASE_P0 + 16, 0)
                    if win.active(-1, TILES):
                        read_out(win, in2, 0, k, BASE_P1, -1)
                        project(win, in2, 1, k, BASE_P1 + 11, -1)
                    if win.active(-2, TILES):
                        read_out(win, join, 1, k, BASE_P2, -2)
                        ffn_input(win, "b", k, BASE_FB, -2, zb[1][win.parity(-2)])
                    if win.active(2, TILES):
                        ffn_input(win, "a", k, BASE_FA, 2, zb[0][win.parity(1)])

            windows(pe, window)


def kernel(**inputs):
    import numpy as np
    import concourse.bacc as bacc
    from concourse.bass_utils import run_bass_kernel_spmd

    a = {k: np.asarray(v) for k, v in inputs.items()}
    b_in = a["L0_attn_b_in"]
    D = b_in.shape[1] // 2

    def turned(w):
        return w.transpose(2, 0, 1).reshape(w.shape[2], -1)

    arrays = dict(
        x=a["L0_attn_x"],
        ln_g=a["L0_attn_ln_g"].T, ln_b=a["L0_attn_ln_b"].T,
        w_in=a["L0_attn_W_in"].transpose(0, 2, 1),
        b_gate=b_in[:, :D].T, b_cand=b_in[:, D:], b_h=a["L0_attn_b_h"],
        w_h=a["L0_attn_W_h"].transpose(0, 2, 1), w_out=a["L0_attn_W_out"].transpose(0, 2, 1),
        b_out=a["L0_attn_b_out"], gate_w=a["L0_ffn_gate_w"].T,
        expert_gate=turned(a["L0_ffn_expert_gate"]), expert_up=turned(a["L0_ffn_expert_up"]),
        expert_down=a["L0_ffn_expert_down"].transpose(0, 2, 1),
        shared_gate=a["L0_ffn_shared_gate"].T, shared_up=a["L0_ffn_shared_up"].T,
        shared_down=a["L0_ffn_shared_down"].T,
    )
    nc = bacc.Bacc("TRN2", target_bir_lowering=False, num_devices=1)
    args, maps = [], {}
    for name, v in arrays.items():
        maps[name] = np.ascontiguousarray(v)
        args.append(nc.dram_tensor(name, v.shape, mybir.dt.from_np(v.dtype), kind="ExternalInput").ap())
    args.append(nc.dram_tensor("out", a["L0_attn_x"].shape, F32, kind="ExternalOutput").ap())
    macaron(nc, *args)
    r = run_bass_kernel_spmd(nc, [maps], core_ids=[0])
    return r.results[0]["out"]
```

```python
from contextlib import ExitStack

import concourse.bass as bass
from concourse import mybir

F32 = mybir.dt.float32
F16 = mybir.dt.float16
U32 = mybir.dt.uint32
ALU = mybir.AluOpType
ACT = mybir.ActivationFunctionType
AX = mybir.AxisListType

P = 128
STEPS = 64
SEQS = 2
TOK = STEPS * SEQS
LAYERS = 2
EXPERTS = 8
FFNS = 1 + EXPERTS
START = (15, 28)
HALVES = 2 * STEPS
JOB0 = -10
SILU, MULTIPLY, DOWN, ACCUMULATE = 4, dict(a=5, b=6), dict(a=7, b=8), dict(a=10, b=11)
BASE_P0, BASE_P1, BASE_P2, BASE_FB, BASE_FA = 0, 31, 58, 63, 94
EPS = 1e-5
GUARD = 1e-20
X_SCALE = 16.0
W_SCALE = 64.0
UNSCALE = 1.0 / (X_SCALE * W_SCALE)

IN1 = dict(
    dve=["stats_x", "moments_x", "y", "stats_y", "moments_y", "normed"],
    pool=["eps_x", "rstd_x", "biased", "eps_y", "rstd_y", "gate", "saved"],
    pe=["turned", "projected"],
    act=["affine", "gate_tanh"])
IN2 = dict(
    dve=["y", "stats_y", "moments_y", "normed"],
    pool=["biased", "eps_y", "rstd_y", "gate"],
    pe=["read_out", "turned", "projected"],
    act=["affine", "gate_tanh"])
JOIN = dict(dve=["y", "x"], pool=[], pe=["read_out"], act=[])
FFN_IN = dict(
    dve=["stats", "moments", "normed", "low", "top_logit", "total", "inv_total", "top_probs",
         "top_index", "inv_pair"],
    pool=["eps", "rstd", "shifted", "exps", "probs", "pair", "guarded", "weights", "index_f",
          "first", "second", "mix"],
    pe=["turned", "logits"],
    act=["high", "full", "logits_copied"])


class Window:

    def __init__(self, eng, static=None, pair=None, shift=0, products=None,
                 constants=None):
        self.constants = constants
        self.eng, self.static, self.pair, self.shift = eng, static, pair, shift
        self.products = products

    def parity(self, d):
        return (self.static + d) % 2 if self.static is not None else (self.shift + d) % 2

    def tile(self, d):
        return self.static + d if self.static is not None else self.pair * 2 + (self.shift + d)

    def active(self, d, tiles):
        return self.static is None or 0 <= self.static + d < tiles

    def count(self, per, d, c, layer=0):
        if self.static is not None:
            return max(per * (self.static + d) + c, 0)
        if (per, layer) not in self.products:
            self.products[per, layer] = self.pair * (2 * per)
        return self.products[per, layer] + (per * (self.shift + d) + c)

    def apart(self, value):
        if self.static is not None:
            return value
        value = self.eng.to_reg(value)
        self.eng.wait_ge(self.constants, 1)
        return value


class Stage:

    def __init__(self, steps, sems):
        self.steps, self.sem = steps, sems

    def past(self, win, eng, step, d):
        steps = self.steps[eng]
        return win.count(len(steps), d, steps.index(step) + 1)


def macaron(nc, x, ln_g, ln_b, w_in, b_in, b_vh, b_h_row, w_h, w_out, b_out, gate_w, expert_gate,
            expert_up, expert_down, shared_gate, shared_up, shared_down, out):
    T = x.shape[1]
    TILES = T // STEPS
    F = shared_down.shape[0]
    CHUNKS = -(-F // P)
    CH = [min(P, F - c * P) for c in range(CHUNKS)]
    JOBS = FFNS * CHUNKS
    FIRST, LAST = -2, TILES + 2
    LOOP = (4, TILES - 2)

    with ExitStack() as ctx:
        def sb(name, shape, dt=F32):
            return ctx.enter_context(nc.sbuf_tensor(name, shape, dt))

        def sem(name):
            return ctx.enter_context(nc.semaphore(name))

        w32 = [sb(f"w32_{g}", [P, FFNS * F]) for g in range(2)]
        w_hi = [sb(f"w_hi{g}", [P, FFNS * F], F16) for g in range(2)]
        w_lo = [sb(f"w_lo{g}", [P, FFNS * F], F16) for g in range(2)]
        wd = sb("wd", [P, JOBS, P])
        wi = sb("wi", [P, LAYERS, 2 * P])
        wh = sb("wh", [P, LAYERS, P])
        wo = sb("wo", [P, LAYERS, P])
        gw = sb("gw", [P, EXPERTS])
        lng = sb("lng", [P, LAYERS])
        lnb = sb("lnb", [P, LAYERS])
        bu = sb("bu", [P, LAYERS])
        half_bu = sb("half_bu", [P, LAYERS])
        bv_row = sb("bv_row", [P, LAYERS, P])
        bh_row = sb("bh_row", [1, LAYERS, P])
        bo = sb("bo", [P, LAYERS, P])
        ones = sb("ones", [P, TOK])
        ident = sb("ident", [P, P])
        experts = sb("experts", [P, EXPERTS])
        minus_half = sb("minus_half", [P, 1])
        euler = sb("euler", [P, EXPERTS])

        x0 = [sb(f"x0_{q}", [TOK, P]) for q in range(2)]
        acc_a = [sb(f"acc_a{q}", [TOK, P]) for q in range(2)]
        x1 = [sb(f"x1_{q}", [TOK, P]) for q in range(2)]
        x2 = [sb(f"x2_{q}", [TOK, P]) for q in range(2)]
        acc_b = [sb(f"acc_b{q}", [TOK, P]) for q in range(2)]
        xs = [sb(f"xs{q}", [P, 2, 2 * TOK], F16) for q in range(2)]
        comb = {h: [sb(f"comb_{h}{q}", [TOK, EXPERTS]) for q in range(2)] for h in "ab"}
        silu = [sb(f"silu{q}", [P, 2 * TOK]) for q in range(2)]
        hidden = [sb(f"hidden{q}", [P, 2 * TOK]) for q in range(2)]
        y0b = [sb(f"y0b{q}", [TOK, P]) for q in range(2)]
        y1b = [sb(f"y1b{q}", [TOK, P]) for q in range(2)]
        y0 = sb("y0", [TOK, P])
        y1 = sb("y1", [TOK, P])
        y2 = sb("y2", [TOK, P])
        hist = [[sb(f"hist{l}{q}", [P, TOK, 5]) for q in range(2)] for l in range(LAYERS)]
        gates = [[sb(f"gates{l}{q}", [P, TOK, 5]) for q in range(2)] for l in range(LAYERS)]
        u_tanh = [sb(f"u_tanh{l}", [P, TOK]) for l in range(LAYERS)]
        xn = [sb(f"xn{l}", [TOK, P]) for l in range(LAYERS)]
        xaT = [sb(f"xaT{l}", [P, TOK]) for l in range(LAYERS)]
        st = {s: sb(f"st_{s}", [TOK, 6]) for s in ("x", "y0", "y1", "fa", "fb")}
        mv = {s: sb(f"mv_{s}", [TOK, 2]) for s in ("x", "y0", "y1", "fa", "fb")}
        ve = {s: sb(f"ve_{s}", [TOK, 1]) for s in ("x", "y0", "y1", "fa", "fb")}
        rs = {s: sb(f"rs_{s}", [TOK, 1]) for s in ("x", "y0", "y1", "fa", "fb")}
        fn = {h: sb(f"fn_{h}", [TOK, P]) for h in "ab"}
        fT = {h: sb(f"fT_{h}", [P, TOK]) for h in "ab"}
        rt = {h: {n: sb(f"rt_{n}_{h}", [TOK, w], U32 if n == "index" else F32)
                  for n, w in dict(logits=8, top=8, shifted=8, exps=8, total=1, inv=1, probs=8,
                                   ptop=8, index=8, pair=1, guarded=1, ipair=1, weights=2,
                                   index_f=2, first=8, second=8).items()} for h in "ab"}

        zb = [[ctx.enter_context(nc.psum_tensor(f"zb{l}{q}", [P, 512], F32)) for q in range(2)]
              for l in range(LAYERS)]
        gu = [ctx.enter_context(nc.psum_tensor(f"gu{q}", [P, 2, 2 * TOK], F32)) for q in range(2)]
        dn = [ctx.enter_context(nc.psum_tensor(f"dn{q}", [P, 512], F32)) for q in range(2)]

        w_loaded = sem("w_loaded")
        GROUPS = ((0, 1), (1, 1 + EXPERTS // 2), (1 + EXPERTS // 2, FFNS))
        g_loaded = [sem(f"g_loaded{n}") for n in range(len(GROUPS))]
        d_loaded = [sem(f"d_loaded{n}") for n in range(2)]
        x_loaded = sem("x_loaded")
        out_stored = sem("out_stored")
        consts_dve = sem("consts_dve")
        consts_pool = sem("consts_pool")
        hi_made = sem("hi_made")
        lo_made = sem("lo_made")
        z_ready = [sem(f"z_ready{l}") for l in range(LAYERS)]
        c_ready = [sem(f"c_ready{l}") for l in range(LAYERS)]
        h_ready = [sem(f"h_ready{l}") for l in range(LAYERS)]
        gu_ready = sem("gu_ready")
        silu_ready = sem("silu_ready")
        hid_ready = {h: sem(f"hid_ready_{h}") for h in "ab"}
        dn_ready = sem("dn_ready")
        acc_done = {h: sem(f"acc_done_{h}") for h in "ab"}

        def stage(name, steps):
            return Stage(steps, {e: sem(f"{name}_{e}") for e, s in steps.items() if s})

        in1, in2, join = stage("in1", IN1), stage("in2", IN2), stage("join", JOIN)
        ffn_in = {h: stage(f"ffn_in_{h}", FFN_IN) for h in "ab"}

        block = ctx.enter_context(nc.Block())

        def windows(eng, run):
            for n in range(FIRST, LOOP[0]):
                run(Window(eng, static=n))
            steps2 = eng.alloc_register(f"steps2_{eng.engine.name}")
            eng.reg_mov(steps2, STEPS * LOOP[0])
            with eng.Fori(LOOP[0] // 2, LOOP[1] // 2) as pair:
                products = {(STEPS, 1): eng.snap(steps2)}
                eng.reg_add(steps2, steps2, 2 * STEPS)
                for shift in range(2):
                    run(Window(eng, pair=pair, shift=shift, products=products,
                               constants=consts_dve))
            for n in range(LOOP[1], LAST + 1):
                run(Window(eng, static=n))

        def rnn_step(win, l, slot):
            d = -l if slot >= START[l] else -1 - l
            return (d, (slot - START[l]) % STEPS) if win.active(d, TILES) else None

        begin = [JOB0 + j * HALVES // JOBS for j in range(JOBS)]

        def jobs_at(win, k, lag):
            for w in range(2):
                if k - w * HALVES - lag in begin and halves(win, w):
                    yield begin.index(k - w * HALVES - lag), w, halves(win, w)

        def halves(win, w):
            return [(h, d) for h, d in (("a", w + 1), ("b", w - 3)) if win.active(d, TILES)]

        def span(on):
            return slice(0 if on[0][0] == "a" else TOK, 2 * TOK if on[-1][0] == "b" else TOK)

        def at_step(buf, t):
            return buf[:, SEQS * t:SEQS * (t + 1), :].rearrange("p s c -> p (s c)")

        cols = {"a": slice(0, TOK), "b": slice(TOK, 2 * TOK)}
        rows = [slice(e * F + c * P, e * F + c * P + CH[c]) for e in range(FFNS) for c in range(CHUNKS)]

        @block.sync
        def _(sp):
            for dst, src in ((wi, w_in), (wh, w_h), (wo, w_out)):
                sp.dma_start(dst[:], src.rearrange("l d e -> d l e")).then_inc(w_loaded, 16)
            sp.dma_start(gw[:], gate_w).then_inc(w_loaded, 16)
            sp.dma_start(lng[:], ln_g).then_inc(w_loaded, 16)
            sp.dma_start(lnb[:], ln_b).then_inc(w_loaded, 16)
            sp.dma_start(bu[:], b_in).then_inc(w_loaded, 16)
            sp.wait_ge(consts_dve, 1)
            sp.dma_start(bv_row[0:1, :, :], b_vh.rearrange("(a l) d -> a l d", a=1)).then_inc(w_loaded, 16)
            sp.dma_start(bh_row[:], b_h_row.rearrange("(a l) d -> a l d", a=1)).then_inc(w_loaded, 16)
            for l in range(LAYERS):
                sp.dma_start(bo[:, l, :], b_out[l, :].partition_broadcast(P)).then_inc(w_loaded, 16)
            for n, (a, b) in enumerate(GROUPS):
                for g, shared, routed in ((0, shared_gate, expert_gate), (1, shared_up, expert_up)):
                    src = shared if n == 0 else routed[:, (a - 1) * F:(b - 1) * F]
                    sp.dma_start(w32[g][:, a * F:b * F], src).then_inc(g_loaded[n], 16)
            whole = F // P
            wd_v = wd[:].rearrange("p (e c) d -> p e c d", c=CHUNKS)
            sp.dma_start(wd_v[:, 0, 0:whole, :],
                         shared_down[0:whole * P, :].rearrange("(c p) d -> p c d", p=P))\
              .then_inc(d_loaded[0], 16)
            sp.dma_start(wd_v[0:CH[-1], 0, CHUNKS - 1, :], shared_down[F - CH[-1]:F, :])\
              .then_inc(d_loaded[0], 16)
            for c in range(CHUNKS):
                sp.dma_start(wd_v[0:CH[c], 1:FFNS, c, :],
                             expert_down[:, c * P:c * P + CH[c], :].rearrange("e p d -> p e d"))\
                  .then_inc(d_loaded[1], 16)

            def window(win):
                d = 2
                if win.active(d, TILES):
                    sp.wait_ge(acc_done["a"], win.apart(win.count(FFNS, 0, 1)))
                    sp.wait_ge(ffn_in["a"].sem["dve"], win.apart(ffn_in["a"].past(win, "dve", "normed", d - 1)))
                    for s in range(SEQS):
                        t = win.tile(d)
                        src = x[s, bass.ds(t * STEPS, STEPS), :]
                        sp.dma_start(x0[win.parity(d)][s:TOK:SEQS, :], src)\
                          .then_inc(x_loaded, 16)
                d = -3
                if win.active(d, TILES):
                    sp.wait_ge(acc_done["b"], win.apart(win.count(FFNS, d, FFNS)))
                    sp.wait_ge(out_stored, win.apart(win.count(32, d, 0)))
                    for s in range(SEQS):
                        t = win.tile(d)
                        dst = out[s, bass.ds(t * STEPS, STEPS), :]
                        sp.dma_start(dst, acc_b[win.parity(d)][s:TOK:SEQS, :])\
                          .then_inc(out_stored, 16)

            windows(sp, window)
            sp.wait_ge(out_stored, 32 * TILES)

        @block.gpsimd
        def _(pool):
            pool.memset(ident[:], 0.0).then_inc(consts_pool, 1)
            pool.memset(minus_half[:], -0.5).then_inc(consts_pool, 1)
            pool.memset(euler[:], 2.718281828459045).then_inc(consts_pool, 1)
            pool.iota(experts[:], pattern=[[1, EXPERTS]], base=0, channel_multiplier=0,
                      allow_small_or_imprecise_dtypes=True).then_inc(consts_pool, 1)
            pool.wait_ge(consts_pool, 4)
            pool.affine_select(out=ident[:], in_=ident[:], compare_op=ALU.not_equal, fill=1.0,
                               base=0, pattern=[[-1, P]], channel_multiplier=1)\
                .then_inc(consts_pool, 1)
            pool.wait_ge(w_loaded, 16 * 11)
            pool.wait_ge(consts_dve, 4)

            def rstd(win, stg, name, d, moments, suffix=""):
                pool.wait_ge(stg.sem["dve"], win.apart(stg.past(win, "dve", moments, d)))
                pool.tensor_scalar(ve[name][:], mv[name][:, 1:2], EPS, None, ALU.add).then_inc(stg.sem["pool"], 1)
                pool.wait_ge(stg.sem["pool"], win.apart(stg.past(win, "pool", "eps" + suffix, d)))
                pool.tensor_tensor(rs[name][:], ve[name][:], minus_half[:], ALU.pow).then_inc(stg.sem["pool"], 1)

            def gate_less_one(win, stg, l, d):
                q = win.parity(d)
                pool.wait_ge(stg.sem["act"], win.apart(stg.past(win, "act", "gate_tanh", d)))
                pool.tensor_scalar(gates[l][q][:, :, 2], u_tanh[l][:], 0.5, -0.5, ALU.mult, ALU.add).then_inc(stg.sem["pool"], 1)

            def route(win, h, d, q):
                stg, r = ffn_in[h], rt[h]
                pool.wait_ge(stg.sem["dve"], win.apart(stg.past(win, "dve", "top_logit", d)))
                pool.tensor_scalar(r["shifted"][:], r["logits"][:], r["top"][:, 0:1], None,
                                       ALU.subtract).then_inc(stg.sem["pool"], 1)
                pool.wait_ge(stg.sem["pool"], win.apart(stg.past(win, "pool", "shifted", d)))
                pool.tensor_tensor(r["exps"][:], euler[:], r["shifted"][:], ALU.pow).then_inc(stg.sem["pool"], 1)
                pool.wait_ge(stg.sem["dve"], win.apart(stg.past(win, "dve", "inv_total", d)))
                pool.tensor_scalar(r["probs"][:], r["exps"][:], r["inv"][:], None, ALU.mult).then_inc(stg.sem["pool"], 1)
                pool.wait_ge(stg.sem["dve"], win.apart(stg.past(win, "dve", "top_probs", d)))
                pool.tensor_tensor(r["pair"][:], r["ptop"][:, 0:1], r["ptop"][:, 1:2], ALU.add).then_inc(stg.sem["pool"], 1)
                pool.wait_ge(stg.sem["pool"], win.apart(stg.past(win, "pool", "pair", d)))
                pool.tensor_scalar(r["guarded"][:], r["pair"][:], GUARD, None, ALU.add).then_inc(stg.sem["pool"], 1)
                pool.wait_ge(stg.sem["dve"], win.apart(stg.past(win, "dve", "inv_pair", d)))
                pool.tensor_scalar(r["weights"][:], r["ptop"][:, 0:2], r["ipair"][:], 0.5,
                                       ALU.mult, ALU.mult).then_inc(stg.sem["pool"], 1)
                pool.tensor_copy(r["index_f"][:], r["index"][:, 0:2]).then_inc(stg.sem["pool"], 1)
                pool.wait_ge(stg.sem["pool"], win.apart(stg.past(win, "pool", "index_f", d)))
                for n, name in enumerate(("first", "second")):
                    pool.tensor_scalar(r[name][:], experts[:], r["index_f"][:, n:n + 1],
                                           r["weights"][:, n:n + 1], ALU.is_equal, ALU.mult).then_inc(stg.sem["pool"], 1)
                pool.wait_ge(stg.sem["pool"], win.apart(stg.past(win, "pool", "second", d)))
                pool.tensor_tensor(comb[h][q][:], r["first"][:], r["second"][:], ALU.add).then_inc(stg.sem["pool"], 1)

            def window(win):
                d = 0
                if win.active(d, TILES):
                    rstd(win, in1, "x", d, "moments_x", "_x")
                    pool.wait_ge(in1.sem["dve"], win.apart(in1.past(win, "dve", "y", d)))
                    pool.tensor_tensor(y0b[win.parity(d)][:], y0[:], bo[:, 0, :], ALU.add).then_inc(in1.sem["pool"], 1)
                    rstd(win, in1, "y0", d, "moments_y", "_y")
                    gate_less_one(win, in1, 0, d)
                d = -1
                if win.active(d, TILES):
                    pool.wait_ge(in2.sem["dve"], win.apart(in2.past(win, "dve", "y", d)))
                    pool.tensor_tensor(y1b[win.parity(d)][:], y1[:], bo[:, 1, :], ALU.add).then_inc(in2.sem["pool"], 1)
                    rstd(win, in2, "y1", d, "moments_y", "_y")
                    gate_less_one(win, in2, 1, d)
                d = 0
                if win.active(d, TILES):
                    pool.wait_ge(join.sem["dve"], win.apart(join.past(win, "dve", "x", d - 2)))
                    pool.tensor_copy(x1[win.parity(d)][:], acc_a[win.parity(d)][:]).then_inc(in1.sem["pool"], 1)
                for h, d in (("b", -2), ("a", 2)):
                    if win.active(d, TILES):
                        rstd(win, ffn_in[h], "f" + h, d, "moments")
                        route(win, h, d, win.parity(1))

            windows(pool, window)

        @block.scalar
        def _(act):
            for e in range(FFNS):
                for n, (a, b) in enumerate(GROUPS):
                    if e == a:
                        act.wait_ge(g_loaded[n], 32)
                for g in range(2):
                    act.activation(w_hi[g][:, e * F:(e + 1) * F], w32[g][:, e * F:(e + 1) * F],
                                   ACT.Copy, scale=W_SCALE).then_inc(hi_made, 1)
            act.wait_ge(consts_dve, 4)

            def drive_in(win, stg, l, k, base, d):
                q = win.parity(d)
                if k == base:
                    act.wait_ge(stg.sem["pe"], stg.past(win, "pe", "turned", d))
                    act.activation(xaT[l][:], zb[l][q][:, 3 * TOK:4 * TOK], ACT.Identity,
                                       scale=lng[:, l:l + 1], bias=lnb[:, l:l + 1]).then_inc(stg.sem["act"], 1)
                if k == base + 6:
                    act.wait_ge(stg.sem["pe"], stg.past(win, "pe", "projected", d))
                    act.activation(u_tanh[l][:], zb[l][q][:, TOK:2 * TOK], ACT.Tanh, scale=0.5,
                                       bias=half_bu[:, l:l + 1]).then_inc(stg.sem["act"], 1)

            def ffn_input(win, h, k, base, d, bank):
                stg = ffn_in[h]
                if k == base + 12:
                    act.wait_ge(stg.sem["pe"], stg.past(win, "pe", "turned", d))
                    act.activation(xs[win.parity(1)][:, 0, cols[h]], bank[:, 3 * TOK:4 * TOK],
                                       ACT.Copy, scale=X_SCALE).then_inc(stg.sem["act"], 1)
                if k == base + 13:
                    act.activation(fT[h][:], bank[:, 3 * TOK:4 * TOK], ACT.Copy).then_inc(stg.sem["act"], 1)
                if k == base + 17:
                    act.wait_ge(stg.sem["pe"], stg.past(win, "pe", "logits", d))
                    act.activation(rt[h]["logits"][:], bank[:, 2 * TOK:2 * TOK + EXPERTS],
                                       ACT.Copy).then_inc(stg.sem["act"], 1)

            def window(win):
                for k in range(HALVES):
                    l = k % 2
                    at = rnn_step(win, l, k // 2)
                    if at:
                        d, t = at
                        act.wait_ge(z_ready[l], win.count(STEPS, d, t + 1, l))
                        z = zb[l][win.parity(d)][:, SEQS * t:SEQS * (t + 1)]
                        pd, pt = (d, t - 1) if t else (d - 1, STEPS - 1)
                        act.activation(
                            hist[l][win.parity(pd)][:, SEQS * pt:SEQS * (pt + 1), 3:5],
                            z.unsqueeze(2).to_broadcast([P, SEQS, 2]), ACT.Tanh, scale=-1.0)\
                           .then_inc(c_ready[l], 1)
                    for j, w, on in jobs_at(win, k, SILU):
                        n, c = CH[j % CHUNKS], span(on)
                        act.wait_ge(gu_ready, win.count(JOBS, w + 1, j + 1))
                        act.activation(silu[win.parity(w + j)][0:n, c], gu[win.parity(w + j)][0:n, 0, c], ACT.Silu,
                                       scale=UNSCALE).then_inc(silu_ready, 1)
                    if win.active(0, TILES):
                        drive_in(win, in1, 0, k, BASE_P0 + 19, 0)
                    if win.active(-1, TILES):
                        drive_in(win, in2, 1, k, BASE_P1 + 16, -1)
                    if win.active(-2, TILES):
                        ffn_input(win, "b", k, BASE_FB, -2, zb[1][win.parity(-2)])
                    if win.active(2, TILES):
                        ffn_input(win, "a", k, BASE_FA, 2, zb[0][win.parity(1)])

            windows(act, window)

        @block.vector
        def _(dve):
            for l in range(LAYERS):
                for q in range(2):
                    dve.memset(gates[l][q][:], 0.0)
                    dve.memset(hist[l][q][:], 0.0)
            for q in range(2):
                dve.memset(hidden[q][:], 0.0)
                dve.memset(xs[q][:], 0.0)
            dve.memset(bv_row[:], 0.0).then_inc(consts_dve, 1)
            dve.memset(ones[:], 1.0).then_inc(consts_dve, 1)
            dve.wait_ge(consts_dve, 1)
            for l in range(LAYERS):
                for q in range(2):
                    dve.memset(gates[l][q][:, :, 1], 1.0)
            dve.wait_ge(w_loaded, 16 * 11)
            dve.tensor_scalar(half_bu[:], bu[:], 0.5, None, ALU.mult).then_inc(consts_dve, 1)
            dve.tensor_tensor(bv_row[0:1, :, :], bv_row[0:1, :, :], bh_row[:], ALU.add)\
               .then_inc(consts_dve, 1)

            def normalise(dst, src, name):
                return dve.tensor_scalar(dst[:], src[:], mv[name][:, 0:1], rs[name][:, 0:1],
                                         ALU.subtract, ALU.mult)

            def in_1(win, k, d):
                if k == BASE_P0:
                    dve.wait_ge(acc_done["a"], win.count(FFNS, d, FFNS))
                    dve.bn_stats(st["x"][:], acc_a[win.parity(d)][:]).then_inc(in1.sem["dve"], 1)
                if k == BASE_P0 + 1:
                    dve.wait_ge(in1.sem["dve"], win.apart(in1.past(win, "dve", "stats_x", d)))
                    dve.bn_aggr(mv["x"][:], st["x"][:]).then_inc(in1.sem["dve"], 1)
                if k == BASE_P0 + 8:
                    dve.wait_ge(in1.sem["pool"], in1.past(win, "pool", "rstd_x", d))
                    normalise(y0, acc_a[win.parity(d)], "x").then_inc(in1.sem["dve"], 1)
                if k == BASE_P0 + 9:
                    dve.wait_ge(in1.sem["dve"], in1.past(win, "dve", "y", d))
                    dve.bn_stats(st["y0"][:], y0[:]).then_inc(in1.sem["dve"], 1)
                if k == BASE_P0 + 10:
                    dve.wait_ge(in1.sem["dve"], win.apart(in1.past(win, "dve", "stats_y", d)))
                    dve.bn_aggr(mv["y0"][:], st["y0"][:]).then_inc(in1.sem["dve"], 1)
                if k == BASE_P0 + 16:
                    dve.wait_ge(in1.sem["pool"], in1.past(win, "pool", "rstd_y", d))
                    normalise(xn[0], y0, "y0").then_inc(in1.sem["dve"], 1)

            def in_2(win, k, d):
                if k == BASE_P1 + 3:
                    dve.wait_ge(in2.sem["pe"], in2.past(win, "pe", "read_out", d))
                    dve.wait_ge(in1.sem["pool"], in1.past(win, "pool", "biased", d))
                    dve.tensor_tensor(y1[:], zb[1][win.parity(d)][:, 2 * TOK:3 * TOK],
                                      y0b[win.parity(d)][:], ALU.add).then_inc(in2.sem["dve"], 1)
                if k == BASE_P1 + 4:
                    dve.wait_ge(in2.sem["dve"], in2.past(win, "dve", "y", d))
                    dve.bn_stats(st["y1"][:], y1[:]).then_inc(in2.sem["dve"], 1)
                if k == BASE_P1 + 5:
                    dve.wait_ge(in2.sem["dve"], win.apart(in2.past(win, "dve", "stats_y", d)))
                    dve.bn_aggr(mv["y1"][:], st["y1"][:]).then_inc(in2.sem["dve"], 1)
                if k == BASE_P1 + 12:
                    dve.wait_ge(in2.sem["pool"], in2.past(win, "pool", "rstd_y", d))
                    normalise(xn[1], y1, "y1").then_inc(in2.sem["dve"], 1)

            def join_x(win, k, d):
                if k == BASE_P2 + 2:
                    dve.wait_ge(join.sem["pe"], join.past(win, "pe", "read_out", d))
                    dve.wait_ge(in2.sem["pool"], in2.past(win, "pool", "biased", d))
                    dve.tensor_tensor(y2[:], zb[1][win.parity(d)][:, 2 * TOK:3 * TOK],
                                      y1b[win.parity(d)][:], ALU.add).then_inc(join.sem["dve"], 1)
                if k == BASE_P2 + 3:
                    dve.wait_ge(join.sem["dve"], join.past(win, "dve", "y", d))
                    dve.wait_ge(in1.sem["pool"], in1.past(win, "pool", "saved", d))
                    dve.tensor_tensor(x2[win.parity(d)][:], y2[:], x1[win.parity(d)][:], ALU.add).then_inc(join.sem["dve"], 1)

            def ffn_input(win, h, k, base, d):
                stg, r, name = ffn_in[h], rt[h], "f" + h
                src = (x0 if h == "a" else x2)[win.parity(d)]
                if k == base:
                    if h == "a":
                        dve.wait_ge(x_loaded, win.count(32, d, 32))
                    else:
                        dve.wait_ge(join.sem["dve"], join.past(win, "dve", "x", d))
                    dve.bn_stats(st[name][:], src[:]).then_inc(stg.sem["dve"], 1)
                if k == base + 1:
                    dve.wait_ge(stg.sem["dve"], win.apart(stg.past(win, "dve", "stats", d)))
                    dve.bn_aggr(mv[name][:], st[name][:]).then_inc(stg.sem["dve"], 1)
                if k == base + 8:
                    dve.wait_ge(stg.sem["pool"], stg.past(win, "pool", "rstd", d))
                    normalise(fn[h], src, name).then_inc(stg.sem["dve"], 1)
                if k == base + 15:
                    dve.wait_ge(stg.sem["act"], stg.past(win, "act", "full", d))
                    dve.scalar_tensor_tensor(
                        out=xs[win.parity(1)][:, 1, cols[h]], in0=fT[h][:], scalar=X_SCALE,
                        in1=xs[win.parity(1)][:, 0, cols[h]], op0=ALU.mult, op1=ALU.subtract).then_inc(stg.sem["dve"], 1)
                if k == base + 18:
                    dve.wait_ge(stg.sem["act"], win.apart(stg.past(win, "act", "logits_copied", d)))
                    dve.max(r["top"][:], r["logits"][:]).then_inc(stg.sem["dve"], 1)
                if k == base + 25:
                    dve.wait_ge(stg.sem["pool"], stg.past(win, "pool", "exps", d))
                    dve.tensor_reduce(r["total"][:], r["exps"][:], AX.X, ALU.add).then_inc(stg.sem["dve"], 1)
                if k == base + 26:
                    dve.wait_ge(stg.sem["dve"], stg.past(win, "dve", "total", d))
                    dve.reciprocal(r["inv"][:], r["total"][:]).then_inc(stg.sem["dve"], 1)
                if k == base + 28:
                    dve.wait_ge(stg.sem["pool"], win.apart(stg.past(win, "pool", "probs", d)))
                    dve.max(r["ptop"][:], r["probs"][:]).then_inc(stg.sem["dve"], 1)
                if k == base + 29:
                    dve.wait_ge(stg.sem["dve"], win.apart(stg.past(win, "dve", "top_probs", d)))
                    dve.max_index(r["index"][:], r["ptop"][:], r["probs"][:]).then_inc(stg.sem["dve"], 1)
                if k == base + 32:
                    dve.wait_ge(stg.sem["pool"], stg.past(win, "pool", "guarded", d))
                    dve.reciprocal(r["ipair"][:], r["guarded"][:]).then_inc(stg.sem["dve"], 1)

            def split_low(e):
                for g in range(2):
                    dve.wait_ge(hi_made, 2 * e + g + 1)
                    part = slice(e * F, (e + 1) * F)
                    dve.scalar_tensor_tensor(out=w_lo[g][:, part], in0=w32[g][:, part],
                                             scalar=W_SCALE, in1=w_hi[g][:, part], op0=ALU.mult,
                                             op1=ALU.subtract).then_inc(lo_made, 1)

            for e in range(FFNS):
                split_low(e)

            def multiply(win, h, w, j):
                n, c = CH[j % CHUNKS], cols[h]
                dve.wait_ge(silu_ready, win.count(JOBS, w + 1, j + 1))
                dve.scalar_tensor_tensor(out=hidden[win.parity(w + j)][0:n, c], in0=gu[win.parity(w + j)][0:n, 1, c],
                                         scalar=UNSCALE, in1=silu[win.parity(w + j)][0:n, c], op0=ALU.mult,
                                         op1=ALU.mult).then_inc(hid_ready[h], 1)

            def accumulate(win, h, w, d, e):
                src = dn[win.parity(w + e)][:, cols[h]]
                acc = (acc_a if h == "a" else acc_b)[win.parity(d)]
                dve.wait_ge(dn_ready, win.count(FFNS, w + 1, e + 1))
                if e == 0:
                    if h == "a":
                        dve.wait_ge(in1.sem["pool"], in1.past(win, "pool", "saved", d - 2))
                    else:
                        dve.wait_ge(out_stored, win.count(32, d, 0))
                    ins = dve.scalar_tensor_tensor(
                        out=acc[:], in0=src, scalar=0.5, in1=(x0 if h == "a" else x2)[win.parity(d)][:],
                        op0=ALU.mult, op1=ALU.add)
                else:
                    dve.wait_ge(acc_done[h], win.count(FFNS, d, e))
                    if e == 1:
                        dve.wait_ge(ffn_in[h].sem["pool"], ffn_in[h].past(win, "pool", "mix", d))
                    ins = dve.scalar_tensor_tensor(
                        out=acc[:], in0=src, scalar=comb[h][win.parity(w)][:, e - 1:e], in1=acc[:],
                        op0=ALU.mult, op1=ALU.add)
                ins.then_inc(acc_done[h], 1)

            def window(win):
                for k in range(HALVES):
                    l = k % 2
                    at = rnn_step(win, l, k // 2)
                    if at:
                        d, t = at
                        q = win.parity(d)
                        pd, pt = (d, t - 1) if t else (d - 1, STEPS - 1)
                        dve.wait_ge(c_ready[l], win.count(STEPS, d, t + 1, l))
                        if t == 0:
                            dve.wait_ge((in1, in2)[l].sem["pool"], (in1, in2)[l].past(win, "pool", "gate", d))
                        dve.wait_ge(h_ready[l], win.count(STEPS, d, t, l))
                        dve.tensor_tensor_scan(
                            out=at_step(hist[l][q], t)[:, 0:8],
                            data0=at_step(gates[l][q], t)[:, 0:8],
                            data1=at_step(hist[l][win.parity(pd)], pt)[:, 2:10],
                            initial=0.0, op0=ALU.mult, op1=ALU.subtract).then_inc(h_ready[l], 1)
                    for h in "ab":
                        for j, w, on in jobs_at(win, k, MULTIPLY[h]):
                            for hh, d in on:
                                if hh == h:
                                    multiply(win, h, w, j)
                    for h in "ab":
                        for j, w, on in jobs_at(win, k, ACCUMULATE[h]):
                            for hh, d in on:
                                if hh == h and j % CHUNKS == CHUNKS - 1:
                                    accumulate(win, h, w, d, j // CHUNKS)
                    if win.active(0, TILES):
                        in_1(win, k, 0)
                    if win.active(-1, TILES):
                        in_2(win, k, -1)
                    if win.active(-2, TILES):
                        join_x(win, k, -2)
                        ffn_input(win, "b", k, BASE_FB, -2)
                    if win.active(2, TILES):
                        ffn_input(win, "a", k, BASE_FA, 2)

            windows(dve, window)

        @block.tensor
        def _(pe):
            pe.wait_ge(w_loaded, 16 * 11)
            pe.wait_ge(consts_dve, 4)
            pe.wait_ge(consts_pool, 5)

            def project(win, stg, l, k, base, d):
                bank = zb[l][win.parity(d)]
                if k == base:
                    if l == 0 and win.active(d + 1, TILES):
                        pe.wait_ge(ffn_in["a"].sem["act"], ffn_in["a"].past(win, "act", "logits_copied", d + 1))
                    pe.wait_ge(stg.sem["dve"], stg.past(win, "dve", "normed", d))
                    pe.transpose(bank[:, 3 * TOK:4 * TOK], xn[l][:], ident[:]).then_inc(stg.sem["pe"], 1)
                if k == base + 3:
                    pe.wait_ge(stg.sem["act"], stg.past(win, "act", "affine", d))
                    pe.matmul(bank[:, 0:TOK], wi[:, l, P:2 * P], xaT[l][:], start=True, stop=False,
                              skip_group_check=True)
                if k == base + 4:
                    pe.matmul(bank[:, 0:TOK], bv_row[:, l, :], ones[:], start=False, stop=False,
                              skip_group_check=True)
                if k == base + 5:
                    pe.matmul(bank[:, TOK:2 * TOK], wi[:, l, 0:P], xaT[l][:], start=False, stop=True,
                                  skip_group_check=True).then_inc(stg.sem["pe"], 1)

            def read_out(win, stg, l, k, base, d):
                if k == base:
                    q = win.parity(d)
                    if l == 0:
                        pe.wait_ge(ffn_in["b"].sem["act"], ffn_in["b"].past(win, "act", "logits_copied", d - 2))
                    pe.wait_ge(h_ready[l], win.count(STEPS, d, STEPS, l))
                    pe.matmul(zb[1][q][:, 2 * TOK:3 * TOK], hist[l][q][:, :, 2], wo[:, l, :], start=True, stop=True,
                                  skip_group_check=True).then_inc(stg.sem["pe"], 1)

            def ffn_input(win, h, k, base, d, bank):
                stg = ffn_in[h]
                if k == base + 10:
                    pe.wait_ge(stg.sem["dve"], stg.past(win, "dve", "normed", d))
                    pe.transpose(bank[:, 3 * TOK:4 * TOK], fn[h][:], ident[:]).then_inc(stg.sem["pe"], 1)
                if k == base + 15:
                    pe.wait_ge(stg.sem["act"], stg.past(win, "act", "full", d))
                    pe.matmul(bank[:, 2 * TOK:2 * TOK + EXPERTS], fT[h][:], gw[:], start=True,
                                  stop=True, skip_group_check=True).then_inc(stg.sem["pe"], 1)

            def gate_or_up(win, on, w, j, g, passes):
                e, ch = divmod(j, CHUNKS)
                n, c, q = CH[ch], slice(0, 2 * TOK), win.parity(w + j)
                src = xs[win.parity(w)]
                if g == 0 and 0 in passes:
                    for h, d in (("a", w + 1), ("b", w - 3)):
                        if win.active(d, TILES) or (j < 2 and win.static + d == TILES):
                            pe.wait_ge(hid_ready[h], win.count(JOBS, d, j - 1))
                    if j == 0:
                        for h, d in on:
                            pe.wait_ge(ffn_in[h].sem["dve"], ffn_in[h].past(win, "dve", "low", d))
                if win.static is not None and win.static + w == -1 and 0 in passes:
                    pe.wait_ge(lo_made, 2 * e + 2)
                dst = gu[q][0:n, g, c]
                r = rows[j]
                products = ((w_hi, 0), (w_hi, 1), (w_lo, 0), (w_lo, 1))
                last = 3 if g == 0 else 2
                for p in passes:
                    part, low = products[p]
                    mm = pe.matmul(dst, part[g][:, r], src[:, low, c], start=(g == 0 and p == 0),
                                   stop=(p == last), skip_group_check=True)
                if g == 1 and last in passes:
                    mm.then_inc(gu_ready, 1)

            def down(win, on, w, j, h):
                e, ch = divmod(j, CHUNKS)
                n = CH[ch]
                if h == "a" and ch == 0:
                    if win.static is not None and win.static + w == -1 and e < 2:
                        pe.wait_ge(d_loaded[e], 16 * (2 if e == 0 else CHUNKS))
                    for hh, d in (("a", w + 1), ("b", w - 3)):
                        if win.active(d, TILES) or (e < 2 and win.static + d == TILES):
                            pe.wait_ge(acc_done[hh], win.count(FFNS, d, e - 1))
                for hh, d in on:
                    if hh == h:
                        pe.wait_ge(hid_ready[h], win.count(JOBS, d, j + 1))
                mm = pe.matmul(dn[win.parity(w + e)][:, cols[h]], hidden[win.parity(w + j)][0:n, cols[h]],
                               wd[0:n, j, :], start=(ch == 0 and h == "a"),
                               stop=(ch == CHUNKS - 1), skip_group_check=True)
                if ch == CHUNKS - 1 and h == "b":
                    mm.then_inc(dn_ready, 1)

            def window(win):
                for k in range(HALVES):
                    l = k % 2
                    at = rnn_step(win, l, k // 2)
                    if at:
                        d, t = at
                        pd, pt = (d, t - 1) if t else (d - 1, STEPS - 1)
                        if t == 0:
                            pe.wait_ge((in1, in2)[l].sem["act"], (in1, in2)[l].past(win, "act", "gate_tanh", d))
                        pe.wait_ge(h_ready[l], win.count(STEPS, d, t, l))
                        z = zb[l][win.parity(d)][:, SEQS * t:SEQS * (t + 1)]
                        pe.matmul(z, wh[:, l, :], hist[l][win.parity(pd)][:, SEQS * pt:SEQS * (pt + 1), 2], start=False,
                                  stop=True, skip_group_check=True).then_inc(z_ready[l], 1)
                    for lag, g, passes in ((0, 0, (0, 1)), (1, 0, (2, 3)), (2, 1, (0, 1)), (3, 1, (2,))):
                        for j, w, on in jobs_at(win, k, lag):
                            gate_or_up(win, on, w, j, g, passes)
                    for h in "ab":
                        for j, w, on in jobs_at(win, k, DOWN[h]):
                            down(win, on, w, j, h)
                    if win.active(0, TILES):
                        project(win, in1, 0, k, BASE_P0 + 18, 0)
                    if win.active(-1, TILES):
                        read_out(win, in2, 0, k, BASE_P1, -1)
                        project(win, in2, 1, k, BASE_P1 + 15, -1)
                    if win.active(-2, TILES):
                        read_out(win, join, 1, k, BASE_P2, -2)
                        ffn_input(win, "b", k, BASE_FB, -2, zb[1][win.parity(-2)])
                    if win.active(2, TILES):
                        ffn_input(win, "a", k, BASE_FA, 2, zb[0][win.parity(1)])

            windows(pe, window)


def kernel(**inputs):
    import numpy as np
    import concourse.bacc as bacc
    from concourse.bass_utils import run_bass_kernel_spmd

    a = {k: np.asarray(v) for k, v in inputs.items()}
    b_in = a["L0_attn_b_in"]
    D = b_in.shape[1] // 2

    def turned(w):
        return w.transpose(2, 0, 1).reshape(w.shape[2], -1)

    arrays = dict(
        x=a["L0_attn_x"],
        ln_g=a["L0_attn_ln_g"].T, ln_b=a["L0_attn_ln_b"].T,
        w_in=a["L0_attn_W_in"].transpose(0, 2, 1),
        b_gate=b_in[:, :D].T, b_cand=b_in[:, D:], b_h=a["L0_attn_b_h"],
        w_h=a["L0_attn_W_h"].transpose(0, 2, 1), w_out=a["L0_attn_W_out"].transpose(0, 2, 1),
        b_out=a["L0_attn_b_out"], gate_w=a["L0_ffn_gate_w"].T,
        expert_gate=turned(a["L0_ffn_expert_gate"]), expert_up=turned(a["L0_ffn_expert_up"]),
        expert_down=a["L0_ffn_expert_down"].transpose(0, 2, 1),
        shared_gate=a["L0_ffn_shared_gate"].T, shared_up=a["L0_ffn_shared_up"].T,
        shared_down=a["L0_ffn_shared_down"].T,
    )
    nc = bacc.Bacc("TRN2", target_bir_lowering=False, num_devices=1)
    args, maps = [], {}
    for name, v in arrays.items():
        maps[name] = np.ascontiguousarray(v)
        args.append(nc.dram_tensor(name, v.shape, mybir.dt.from_np(v.dtype), kind="ExternalInput").ap())
    args.append(nc.dram_tensor("out", a["L0_attn_x"].shape, F32, kind="ExternalOutput").ap())
    macaron(nc, *args)
    r = run_bass_kernel_spmd(nc, [maps], core_ids=[0])
    return r.results[0]["out"]
```

```python
from contextlib import ExitStack

import concourse.bass as bass
from concourse import mybir

F32 = mybir.dt.float32
F16 = mybir.dt.float16
U32 = mybir.dt.uint32
ALU = mybir.AluOpType
ACT = mybir.ActivationFunctionType
AX = mybir.AxisListType

P = 128
STEPS = 64
SEQS = 2
TOK = STEPS * SEQS
LAYERS = 2
EXPERTS = 8
FFNS = 1 + EXPERTS
START = (13, 24)
HALVES = 2 * STEPS
LEAD_HI, LEAD_LO = 3, 1
JOB0 = -15
SILU, MULTIPLY, DOWN = 4, dict(a=5, b=6), dict(a=8, b=9)
WEIGH, ACCUMULATE = dict(a=10, b=11), dict(a=11, b=12)
BASE_P0, BASE_P1, BASE_P2, BASE_FB, BASE_FA = 0, 27, 50, 55, 90
EPS = 1e-5
GUARD = 1e-20
X_SCALE = 16.0
W_SCALE = 64.0
UNSCALE = 1.0 / (X_SCALE * W_SCALE)

IN1 = dict(
    dve=["stats_x", "moments_x", "y", "stats_y", "moments_y", "normed"],
    pool=["eps_x", "rstd_x", "biased", "eps_y", "rstd_y", "gate", "saved"],
    pe=["turned", "projected"],
    act=["affine", "gate_tanh"])
IN2 = dict(
    dve=["y", "stats_y", "moments_y", "normed"],
    pool=["biased", "eps_y", "rstd_y", "gate"],
    pe=["read_out", "turned", "projected"],
    act=["affine", "gate_tanh"])
JOIN = dict(dve=["y", "x"], pool=[], pe=["read_out"], act=[])
FFN_IN = dict(
    dve=["stats", "moments", "normed", "low", "top_logit", "total", "inv_total", "top_probs",
         "top_index", "inv_pair"],
    pool=["eps", "rstd", "shifted", "exps", "probs", "pair", "guarded", "weights", "index_f",
          "first", "second", "mix"],
    pe=["turned", "logits"],
    act=["high", "full", "logits_copied"])


class Window:

    def __init__(self, eng, static=None, pair=None, shift=0, products=None,
                 constants=None):
        self.constants = constants
        self.eng, self.static, self.pair, self.shift = eng, static, pair, shift
        self.products = products

    def parity(self, d):
        return (self.static + d) % 2 if self.static is not None else (self.shift + d) % 2

    def tile(self, d):
        return self.static + d if self.static is not None else self.pair * 2 + (self.shift + d)

    def active(self, d, tiles):
        return self.static is None or 0 <= self.static + d < tiles

    def count(self, per, d, c, layer=0):
        if self.static is not None:
            return max(per * (self.static + d) + c, 0)
        if (per, layer) not in self.products:
            self.products[per, layer] = self.pair * (2 * per)
        return self.products[per, layer] + (per * (self.shift + d) + c)

    def apart(self, value):
        if self.static is not None:
            return value
        value = self.eng.to_reg(value)
        self.eng.wait_ge(self.constants, 1)
        return value


class Stage:

    def __init__(self, steps, sems):
        self.steps, self.sem = steps, sems

    def past(self, win, eng, step, d):
        steps = self.steps[eng]
        return win.count(len(steps), d, steps.index(step) + 1)


def macaron(nc, x, ln_g, ln_b, w_in, b_in, b_vh, b_h_row, w_h, w_out, b_out, gate_w, expert_gate,
            expert_up, expert_down, shared_gate, shared_up, shared_down, out):
    T = x.shape[1]
    TILES = T // STEPS
    F = shared_down.shape[0]
    CHUNKS = -(-F // P)
    CH = [min(P, F - c * P) for c in range(CHUNKS)]
    JOBS = FFNS * CHUNKS
    FIRST, LAST = -2, TILES + 2
    LOOP = (4, TILES - 2)

    with ExitStack() as ctx:
        def sb(name, shape, dt=F32):
            return ctx.enter_context(nc.sbuf_tensor(name, shape, dt))

        def sem(name):
            return ctx.enter_context(nc.semaphore(name))

        w32 = [sb(f"w32_{g}", [P, FFNS * F]) for g in range(2)]
        w_hi = [sb(f"w_hi{g}", [P, FFNS * F], F16) for g in range(2)]
        w_lo = [sb(f"w_lo{g}", [P, FFNS * F], F16) for g in range(2)]
        wd = sb("wd", [P, JOBS, P])
        wi = sb("wi", [P, LAYERS, 2 * P])
        wh = sb("wh", [P, LAYERS, P])
        wo = sb("wo", [P, LAYERS, P])
        gw = sb("gw", [P, EXPERTS])
        lng = sb("lng", [P, LAYERS])
        lnb = sb("lnb", [P, LAYERS])
        bu = sb("bu", [P, LAYERS])
        half_bu = sb("half_bu", [P, LAYERS])
        bv_row = sb("bv_row", [P, LAYERS, P])
        bh_row = sb("bh_row", [1, LAYERS, P])
        bo = sb("bo", [P, LAYERS, P])
        ones = sb("ones", [P, TOK])
        ident = sb("ident", [P, P])
        experts = sb("experts", [P, EXPERTS])
        minus_half = sb("minus_half", [P, 1])
        euler = sb("euler", [P, EXPERTS])

        x0 = [sb(f"x0_{q}", [TOK, P]) for q in range(2)]
        acc_a = [sb(f"acc_a{q}", [TOK, P]) for q in range(2)]
        x1 = [sb(f"x1_{q}", [TOK, P]) for q in range(2)]
        x2 = [sb(f"x2_{q}", [TOK, P]) for q in range(2)]
        acc_b = [sb(f"acc_b{q}", [TOK, P]) for q in range(2)]
        xs = [sb(f"xs{q}", [P, 2, 2 * TOK], F16) for q in range(2)]
        comb = {h: [sb(f"comb_{h}{q}", [TOK, EXPERTS]) for q in range(2)] for h in "ab"}
        weighted = {h: sb(f"weighted_{h}", [TOK, P]) for h in "ab"}
        silu = [sb(f"silu{q}", [P, 2 * TOK]) for q in range(2)]
        hidden = [sb(f"hidden{q}", [P, 2 * TOK]) for q in range(2)]
        y0b = [sb(f"y0b{q}", [TOK, P]) for q in range(2)]
        y1b = [sb(f"y1b{q}", [TOK, P]) for q in range(2)]
        y0 = sb("y0", [TOK, P])
        y1 = sb("y1", [TOK, P])
        y2 = sb("y2", [TOK, P])
        hist = [[sb(f"hist{l}{q}", [P, TOK, 5]) for q in range(2)] for l in range(LAYERS)]
        gates = [[sb(f"gates{l}{q}", [P, TOK, 5]) for q in range(2)] for l in range(LAYERS)]
        u_tanh = [sb(f"u_tanh{l}", [P, TOK]) for l in range(LAYERS)]
        xn = [sb(f"xn{l}", [TOK, P]) for l in range(LAYERS)]
        xaT = [sb(f"xaT{l}", [P, TOK]) for l in range(LAYERS)]
        st = {s: sb(f"st_{s}", [TOK, 6]) for s in ("x", "y0", "y1", "fa", "fb")}
        mv = {s: sb(f"mv_{s}", [TOK, 2]) for s in ("x", "y0", "y1", "fa", "fb")}
        ve = {s: sb(f"ve_{s}", [TOK, 1]) for s in ("x", "y0", "y1", "fa", "fb")}
        rs = {s: sb(f"rs_{s}", [TOK, 1]) for s in ("x", "y0", "y1", "fa", "fb")}
        fn = {h: sb(f"fn_{h}", [TOK, P]) for h in "ab"}
        fT = {h: sb(f"fT_{h}", [P, TOK]) for h in "ab"}
        rt = {h: {n: sb(f"rt_{n}_{h}", [TOK, w], U32 if n == "index" else F32)
                  for n, w in dict(logits=8, top=8, shifted=8, exps=8, total=1, inv=1, probs=8,
                                   ptop=8, index=8, pair=1, guarded=1, ipair=1, weights=2,
                                   index_f=2, first=8, second=8).items()} for h in "ab"}

        zb = [[ctx.enter_context(nc.psum_tensor(f"zb{l}{q}", [P, 512], F32)) for q in range(2)]
              for l in range(LAYERS)]
        gu = [ctx.enter_context(nc.psum_tensor(f"gu{q}", [P, 2, 2 * TOK], F32)) for q in range(2)]
        dn = [ctx.enter_context(nc.psum_tensor(f"dn{q}", [P, 512], F32)) for q in range(2)]

        w_loaded = sem("w_loaded")
        gw_loaded = sem("gw_loaded")
        G_PARTS = [(0, 1)] + [(e, min(e + 2, FFNS)) for e in range(1, FFNS, 2)]
        D_PARTS = [(0, 1)] + [(e, min(e + 4, FFNS)) for e in range(1, FFNS, 4)]
        g_loaded = [sem(f"g_loaded{n}") for n in range(len(G_PARTS))]
        d_loaded = [sem(f"d_loaded{n}") for n in range(len(D_PARTS))]
        x_loaded = sem("x_loaded")
        out_stored = sem("out_stored")
        consts_dve = sem("consts_dve")
        consts_pool = sem("consts_pool")
        POOL_CONSTS = 17
        hi_made = sem("hi_made")
        lo_made = sem("lo_made")
        z_ready = [sem(f"z_ready{l}") for l in range(LAYERS)]
        c_ready = [sem(f"c_ready{l}") for l in range(LAYERS)]
        h_ready = [sem(f"h_ready{l}") for l in range(LAYERS)]
        gu_ready = sem("gu_ready")
        silu_ready = sem("silu_ready")
        hid_ready = {h: sem(f"hid_ready_{h}") for h in "ab"}
        dn_ready = sem("dn_ready")
        weighted_ready = {h: sem(f"weighted_ready_{h}") for h in "ab"}
        acc_done = {h: sem(f"acc_done_{h}") for h in "ab"}

        def stage(name, steps):
            return Stage(steps, {e: sem(f"{name}_{e}") for e, s in steps.items() if s})

        in1, in2, join = stage("in1", IN1), stage("in2", IN2), stage("join", JOIN)
        ffn_in = {h: stage(f"ffn_in_{h}", FFN_IN) for h in "ab"}

        block = ctx.enter_context(nc.Block())

        def windows(eng, run, first=FIRST):
            for n in range(first, LOOP[0]):
                run(Window(eng, static=n))
            steps2 = eng.alloc_register(f"steps2_{eng.engine.name}")
            eng.reg_mov(steps2, STEPS * LOOP[0])
            with eng.Fori(LOOP[0] // 2, LOOP[1] // 2) as pair:
                products = {(STEPS, 1): eng.snap(steps2)}
                eng.reg_add(steps2, steps2, 2 * STEPS)
                for shift in range(2):
                    run(Window(eng, pair=pair, shift=shift, products=products,
                               constants=consts_dve))
            for n in range(LOOP[1], LAST + 1):
                run(Window(eng, static=n))

        def rnn_step(win, l, slot):
            d = -l if slot >= START[l] else -1 - l
            return (d, (slot - START[l]) % STEPS) if win.active(d, TILES) else None

        begin = [JOB0 + j * HALVES // JOBS for j in range(JOBS)]

        def jobs_at(win, k, lag):
            for w in range(2):
                if k - w * HALVES - lag in begin and halves(win, w):
                    yield begin.index(k - w * HALVES - lag), w, halves(win, w)

        def splits_at(win, k, lead):
            if win.static in (-2, -1):
                for e in range(FFNS):
                    if begin[max(e * CHUNKS - lead, 0)] == k + (win.static + 1) * HALVES:
                        yield e

        def wide(win, w, e):
            n = win.static + w if win.static is not None else 0
            return 0 <= n <= TILES or n == TILES + 1 and e < FFNS // 2 + 1

        def halves(win, w):
            return [(h, d) for h, d in (("a", w + 1), ("b", w - 3)) if win.active(d, TILES)]

        def span(on):
            return slice(0 if on[0][0] == "a" else TOK, 2 * TOK if on[-1][0] == "b" else TOK)

        def at_step(buf, t):
            return buf[:, SEQS * t:SEQS * (t + 1), :].rearrange("p s c -> p (s c)")

        cols = {"a": slice(0, TOK), "b": slice(TOK, 2 * TOK)}
        rows = [slice(e * F + c * P, e * F + c * P + CH[c]) for e in range(FFNS) for c in range(CHUNKS)]

        @block.sync
        def _(sp):
            def window(win):
                d = 2
                if win.active(d, TILES):
                    sp.wait_ge(acc_done["a"], win.apart(win.count(FFNS, 0, 1)))
                    sp.wait_ge(ffn_in["a"].sem["dve"], win.apart(ffn_in["a"].past(win, "dve", "normed", d - 1)))
                    for s in range(SEQS):
                        t = win.tile(d)
                        src = x[s, bass.ds(t * STEPS, STEPS), :]
                        sp.dma_start(x0[win.parity(d)][s:TOK:SEQS, :], src)\
                          .then_inc(x_loaded, 16)
                d = -3
                if win.active(d, TILES):
                    sp.wait_ge(acc_done["b"], win.apart(win.count(FFNS, d, FFNS)))
                    sp.wait_ge(out_stored, win.apart(win.count(32, d, 0)))
                    for s in range(SEQS):
                        t = win.tile(d)
                        dst = out[s, bass.ds(t * STEPS, STEPS), :]
                        sp.dma_start(dst, acc_b[win.parity(d)][s:TOK:SEQS, :])\
                          .then_inc(out_stored, 16)

            window(Window(sp, static=FIRST))
            sp.dma_start(gw[:], gate_w).then_inc(gw_loaded, 16)
            wd_v = wd[:].rearrange("p (e c) d -> p e c d", c=CHUNKS)

            def load_gate_up(n):
                a, b = G_PARTS[n]
                for g, shared, routed in ((0, shared_gate, expert_gate), (1, shared_up, expert_up)):
                    src = shared if n == 0 else routed[:, (a - 1) * F:(b - 1) * F]
                    sp.dma_start(w32[g][:, a * F:b * F], src).then_inc(g_loaded[n], 16)

            def load_down(n):
                a, b = D_PARTS[n]
                if n == 0:
                    whole = F // P
                    sp.dma_start(wd_v[:, 0, 0:whole, :],
                                 shared_down[0:whole * P, :].rearrange("(c p) d -> p c d", p=P))\
                      .then_inc(d_loaded[0], 16)
                    sp.dma_start(wd_v[0:CH[-1], 0, CHUNKS - 1, :], shared_down[F - CH[-1]:F, :])\
                      .then_inc(d_loaded[0], 16)
                else:
                    for c in range(CHUNKS):
                        sp.dma_start(wd_v[0:CH[c], a:b, c, :],
                                     expert_down[a - 1:b - 1, c * P:c * P + CH[c], :].rearrange("e p d -> p e d"))\
                          .then_inc(d_loaded[n], 16)

            for n, (a, b) in enumerate(G_PARTS):
                load_gate_up(n)
                for m, part in enumerate(D_PARTS):
                    if part[0] == a:
                        load_down(m)
            for dst, src in ((wi, w_in), (wh, w_h), (wo, w_out)):
                sp.dma_start(dst[:], src.rearrange("l d e -> d l e")).then_inc(w_loaded, 16)
            sp.dma_start(lng[:], ln_g).then_inc(w_loaded, 16)
            sp.dma_start(lnb[:], ln_b).then_inc(w_loaded, 16)
            sp.dma_start(bu[:], b_in).then_inc(w_loaded, 16)
            sp.wait_ge(consts_dve, 1)
            sp.dma_start(bv_row[0:1, :, :], b_vh.rearrange("(a l) d -> a l d", a=1)).then_inc(w_loaded, 16)
            sp.dma_start(bh_row[:], b_h_row.rearrange("(a l) d -> a l d", a=1)).then_inc(w_loaded, 16)
            for l in range(LAYERS):
                sp.dma_start(bo[:, l, :], b_out[l, :].partition_broadcast(P)).then_inc(w_loaded, 16)

            windows(sp, window, first=FIRST + 1)
            sp.wait_ge(out_stored, 32 * TILES)

        @block.gpsimd
        def _(pool):
            pool.memset(ident[:], 0.0).then_inc(consts_pool, 1)
            pool.memset(minus_half[:], -0.5).then_inc(consts_pool, 1)
            pool.memset(euler[:], 2.718281828459045).then_inc(consts_pool, 1)
            pool.iota(experts[:], pattern=[[1, EXPERTS]], base=0, channel_multiplier=0,
                      allow_small_or_imprecise_dtypes=True).then_inc(consts_pool, 1)
            pool.wait_ge(consts_pool, 4)
            pool.affine_select(out=ident[:], in_=ident[:], compare_op=ALU.not_equal, fill=1.0,
                               base=0, pattern=[[-1, P]], channel_multiplier=1)\
                .then_inc(consts_pool, 1)
            for l in range(LAYERS):
                for q in range(2):
                    pool.memset(gates[l][q][:], 0.0).then_inc(consts_pool, 1)
            for q in range(2):
                pool.memset(hidden[q][:, cols["b"]], 0.0).then_inc(consts_pool, 1)
                pool.memset(xs[q][:, :, cols["b"]], 0.0).then_inc(consts_pool, 1)
            pool.wait_ge(consts_pool, 13)
            for l in range(LAYERS):
                for q in range(2):
                    pool.memset(gates[l][q][:, :, 1], 1.0).then_inc(consts_pool, 1)
            pool.wait_ge(consts_pool, POOL_CONSTS)

            def rstd(win, stg, name, d, moments, suffix=""):
                pool.wait_ge(stg.sem["dve"], win.apart(stg.past(win, "dve", moments, d)))
                pool.tensor_scalar(ve[name][:], mv[name][:, 1:2], EPS, None, ALU.add).then_inc(stg.sem["pool"], 1)
                pool.wait_ge(stg.sem["pool"], win.apart(stg.past(win, "pool", "eps" + suffix, d)))
                pool.tensor_tensor(rs[name][:], ve[name][:], minus_half[:], ALU.pow).then_inc(stg.sem["pool"], 1)

            def gate_less_one(win, stg, l, d):
                q = win.parity(d)
                pool.wait_ge(stg.sem["act"], win.apart(stg.past(win, "act", "gate_tanh", d)))
                pool.tensor_scalar(gates[l][q][:, :, 2], u_tanh[l][:], 0.5, -0.5, ALU.mult, ALU.add).then_inc(stg.sem["pool"], 1)

            def route(win, h, k, base, d, q):
                stg, r = ffn_in[h], rt[h]
                if k == base + 19:
                    pool.wait_ge(stg.sem["dve"], win.apart(stg.past(win, "dve", "top_logit", d)))
                    pool.tensor_scalar(r["shifted"][:], r["logits"][:], r["top"][:, 0:1], None,
                                       ALU.subtract).then_inc(stg.sem["pool"], 1)
                    pool.wait_ge(stg.sem["pool"], win.apart(stg.past(win, "pool", "shifted", d)))
                    pool.tensor_tensor(r["exps"][:], euler[:], r["shifted"][:], ALU.pow).then_inc(stg.sem["pool"], 1)
                if k == base + 27:
                    pool.wait_ge(stg.sem["dve"], win.apart(stg.past(win, "dve", "inv_total", d)))
                    pool.tensor_scalar(r["probs"][:], r["exps"][:], r["inv"][:], None, ALU.mult).then_inc(stg.sem["pool"], 1)
                if k == base + 29:
                    pool.wait_ge(stg.sem["dve"], win.apart(stg.past(win, "dve", "top_probs", d)))
                    pool.tensor_tensor(r["pair"][:], r["ptop"][:, 0:1], r["ptop"][:, 1:2], ALU.add).then_inc(stg.sem["pool"], 1)
                    pool.wait_ge(stg.sem["pool"], win.apart(stg.past(win, "pool", "pair", d)))
                    pool.tensor_scalar(r["guarded"][:], r["pair"][:], GUARD, None, ALU.add).then_inc(stg.sem["pool"], 1)
                if k == base + 33:
                    pool.wait_ge(stg.sem["dve"], win.apart(stg.past(win, "dve", "inv_pair", d)))
                    pool.tensor_scalar(r["weights"][:], r["ptop"][:, 0:2], r["ipair"][:], 0.5,
                                       ALU.mult, ALU.mult).then_inc(stg.sem["pool"], 1)
                    pool.tensor_copy(r["index_f"][:], r["index"][:, 0:2]).then_inc(stg.sem["pool"], 1)
                    pool.wait_ge(stg.sem["pool"], win.apart(stg.past(win, "pool", "index_f", d)))
                    for n, name in enumerate(("first", "second")):
                        pool.tensor_scalar(r[name][:], experts[:], r["index_f"][:, n:n + 1],
                                           r["weights"][:, n:n + 1], ALU.is_equal, ALU.mult).then_inc(stg.sem["pool"], 1)
                    pool.wait_ge(stg.sem["pool"], win.apart(stg.past(win, "pool", "second", d)))
                    pool.tensor_tensor(comb[h][q][:], r["first"][:], r["second"][:], ALU.add).then_inc(stg.sem["pool"], 1)

            def accumulate(win, h, w, d, e):
                acc = (acc_a if h == "a" else acc_b)[win.parity(d)]
                if e == 0:
                    if h == "a":
                        pool.wait_ge(in1.sem["pool"], win.apart(in1.past(win, "pool", "saved", d - 2)))
                    else:
                        pool.wait_ge(out_stored, win.apart(win.count(32, d, 0)))
                pool.wait_ge(acc_done[h], win.apart(win.count(FFNS, d, e)))
                pool.wait_ge(weighted_ready[h], win.apart(win.count(FFNS, d, e + 1)))
                so_far = (x0 if h == "a" else x2)[win.parity(d)] if e == 0 else acc
                pool.tensor_tensor(acc[:], weighted[h][:], so_far[:], ALU.add).then_inc(acc_done[h], 1)

            def in_1(win, k, d):
                if k == BASE_P0 and win.static == 0:
                    pool.wait_ge(w_loaded, 16 * 10)
                if k == BASE_P0 + 2:
                    rstd(win, in1, "x", d, "moments_x", "_x")
                if k == BASE_P0 + 8:
                    pool.wait_ge(in1.sem["dve"], win.apart(in1.past(win, "dve", "y", d)))
                    pool.tensor_tensor(y0b[win.parity(d)][:], y0[:], bo[:, 0, :], ALU.add).then_inc(in1.sem["pool"], 1)
                if k == BASE_P0 + 10:
                    rstd(win, in1, "y0", d, "moments_y", "_y")
                if k == BASE_P0 + 23:
                    gate_less_one(win, in1, 0, d)
                if k == BASE_P2 + 6:
                    pool.wait_ge(join.sem["dve"], win.apart(join.past(win, "dve", "x", d - 2)))
                    pool.tensor_copy(x1[win.parity(d)][:], acc_a[win.parity(d)][:]).then_inc(in1.sem["pool"], 1)

            def in_2(win, k, d):
                if k == BASE_P1 + 4:
                    pool.wait_ge(in2.sem["dve"], win.apart(in2.past(win, "dve", "y", d)))
                    pool.tensor_tensor(y1b[win.parity(d)][:], y1[:], bo[:, 1, :], ALU.add).then_inc(in2.sem["pool"], 1)
                if k == BASE_P1 + 6:
                    rstd(win, in2, "y1", d, "moments_y", "_y")
                if k == BASE_P1 + 20:
                    gate_less_one(win, in2, 1, d)

            def window(win):
                for k in range(HALVES):
                    for h in "ab":
                        for j, w, on in jobs_at(win, k, ACCUMULATE[h]):
                            for hh, d in on:
                                if hh == h and j % CHUNKS == CHUNKS - 1:
                                    accumulate(win, h, w, d, j // CHUNKS)
                    if win.active(0, TILES):
                        in_1(win, k, 0)
                    if win.active(-1, TILES):
                        in_2(win, k, -1)
                    for h, base, d in (("b", BASE_FB, -2), ("a", BASE_FA, 2)):
                        if win.active(d, TILES):
                            if k == base + 2:
                                rstd(win, ffn_in[h], "f" + h, d, "moments")
                            route(win, h, k, base, d, win.parity(1))

            windows(pool, window)

        @block.scalar
        def _(act):
            def split_high(e):
                for n, (a, b) in enumerate(G_PARTS):
                    if e == a:
                        act.wait_ge(g_loaded[n], 32)
                for g in range(2):
                    act.activation(w_hi[g][:, e * F:(e + 1) * F], w32[g][:, e * F:(e + 1) * F],
                                   ACT.Copy, scale=W_SCALE).then_inc(hi_made, 1)

            def drive_in(win, stg, l, k, base, d):
                q = win.parity(d)
                if k == base:
                    act.wait_ge(stg.sem["pe"], stg.past(win, "pe", "turned", d))
                    act.activation(xaT[l][:], zb[l][q][:, 3 * TOK:4 * TOK], ACT.Identity,
                                       scale=lng[:, l:l + 1], bias=lnb[:, l:l + 1]).then_inc(stg.sem["act"], 1)
                if k == base + 5:
                    act.wait_ge(stg.sem["pe"], stg.past(win, "pe", "projected", d))
                    act.activation(u_tanh[l][:], zb[l][q][:, TOK:2 * TOK], ACT.Tanh, scale=0.5,
                                       bias=half_bu[:, l:l + 1]).then_inc(stg.sem["act"], 1)

            def ffn_input(win, h, k, base, d, bank):
                stg = ffn_in[h]
                if k == base + 12:
                    act.wait_ge(stg.sem["pe"], stg.past(win, "pe", "turned", d))
                    act.activation(xs[win.parity(1)][:, 0, cols[h]], bank[:, 3 * TOK:4 * TOK],
                                       ACT.Copy, scale=X_SCALE).then_inc(stg.sem["act"], 1)
                if k == base + 13:
                    act.activation(fT[h][:], bank[:, 3 * TOK:4 * TOK], ACT.Copy).then_inc(stg.sem["act"], 1)
                if k == base + 17:
                    act.wait_ge(stg.sem["pe"], stg.past(win, "pe", "logits", d))
                    act.activation(rt[h]["logits"][:], bank[:, 2 * TOK:2 * TOK + EXPERTS],
                                       ACT.Copy).then_inc(stg.sem["act"], 1)

            def weigh(win, h, w, d, e):
                act.wait_ge(dn_ready, win.count(FFNS, w + 1, e + 1))
                if e == 1:
                    act.wait_ge(ffn_in[h].sem["pool"], ffn_in[h].past(win, "pool", "mix", d))
                act.wait_ge(acc_done[h], win.count(FFNS, d, e))
                weight = 0.5 if e == 0 else comb[h][win.parity(w)][:, e - 1:e]
                act.activation(weighted[h][:], dn[win.parity(w + e)][:, cols[h]], ACT.Copy,
                               scale=weight).then_inc(weighted_ready[h], 1)

            def window(win):
                if win.static == 0:
                    act.wait_ge(consts_dve, 4)
                for k in range(HALVES):
                    l = k % 2
                    for e in splits_at(win, k, LEAD_HI):
                        split_high(e)
                    at = rnn_step(win, l, k // 2)
                    if at:
                        d, t = at
                        act.wait_ge(z_ready[l], win.count(STEPS, d, t + 1, l))
                        z = zb[l][win.parity(d)][:, SEQS * t:SEQS * (t + 1)]
                        pd, pt = (d, t - 1) if t else (d - 1, STEPS - 1)
                        act.activation(
                            hist[l][win.parity(pd)][:, SEQS * pt:SEQS * (pt + 1), 3:5],
                            z.unsqueeze(2).to_broadcast([P, SEQS, 2]), ACT.Tanh, scale=-1.0)\
                           .then_inc(c_ready[l], 1)
                    for h in "ab":
                        for j, w, on in jobs_at(win, k, WEIGH[h]):
                            for hh, d in on:
                                if hh == h and j % CHUNKS == CHUNKS - 1:
                                    weigh(win, h, w, d, j // CHUNKS)
                    for j, w, on in jobs_at(win, k, SILU):
                        n, c = CH[j % CHUNKS], span(on)
                        act.wait_ge(gu_ready, win.count(JOBS, w + 1, j + 1))
                        act.activation(silu[win.parity(w + j)][0:n, c], gu[win.parity(w + j)][0:n, 0, c], ACT.Silu,
                                       scale=UNSCALE).then_inc(silu_ready, 1)
                    if win.active(0, TILES):
                        drive_in(win, in1, 0, k, BASE_P0 + 16, 0)
                    if win.active(-1, TILES):
                        drive_in(win, in2, 1, k, BASE_P1 + 13, -1)
                    if win.active(-2, TILES):
                        ffn_input(win, "b", k, BASE_FB, -2, zb[1][win.parity(-2)])
                    if win.active(2, TILES):
                        ffn_input(win, "a", k, BASE_FA, 2, zb[0][win.parity(1)])

            windows(act, window)

        @block.vector
        def _(dve):
            for l in range(LAYERS):
                dve.memset(at_step(hist[l][1], STEPS - 1), 0.0)
            dve.memset(bv_row[:], 0.0).then_inc(consts_dve, 1)
            dve.memset(ones[:], 1.0).then_inc(consts_dve, 1)

            def biases():
                dve.wait_ge(w_loaded, 16 * 10)
                dve.tensor_scalar(half_bu[:], bu[:], 0.5, None, ALU.mult).then_inc(consts_dve, 1)
                dve.tensor_tensor(bv_row[0:1, :, :], bv_row[0:1, :, :], bh_row[:], ALU.add)\
                   .then_inc(consts_dve, 1)

            def normalise(dst, src, name):
                return dve.tensor_scalar(dst[:], src[:], mv[name][:, 0:1], rs[name][:, 0:1],
                                         ALU.subtract, ALU.mult)

            def in_1(win, k, d):
                if k == BASE_P0:
                    dve.wait_ge(acc_done["a"], win.count(FFNS, d, FFNS))
                    dve.bn_stats(st["x"][:], acc_a[win.parity(d)][:]).then_inc(in1.sem["dve"], 1)
                if k == BASE_P0 + 1:
                    dve.wait_ge(in1.sem["dve"], win.apart(in1.past(win, "dve", "stats_x", d)))
                    dve.bn_aggr(mv["x"][:], st["x"][:]).then_inc(in1.sem["dve"], 1)
                if k == BASE_P0 + 7:
                    dve.wait_ge(in1.sem["pool"], in1.past(win, "pool", "rstd_x", d))
                    normalise(y0, acc_a[win.parity(d)], "x").then_inc(in1.sem["dve"], 1)
                if k == BASE_P0 + 8:
                    dve.wait_ge(in1.sem["dve"], in1.past(win, "dve", "y", d))
                    dve.bn_stats(st["y0"][:], y0[:]).then_inc(in1.sem["dve"], 1)
                if k == BASE_P0 + 9:
                    dve.wait_ge(in1.sem["dve"], win.apart(in1.past(win, "dve", "stats_y", d)))
                    dve.bn_aggr(mv["y0"][:], st["y0"][:]).then_inc(in1.sem["dve"], 1)
                if k == BASE_P0 + 13:
                    dve.wait_ge(in1.sem["pool"], in1.past(win, "pool", "rstd_y", d))
                    normalise(xn[0], y0, "y0").then_inc(in1.sem["dve"], 1)

            def in_2(win, k, d):
                if k == BASE_P1 + 3:
                    dve.wait_ge(in2.sem["pe"], in2.past(win, "pe", "read_out", d))
                    dve.wait_ge(in1.sem["pool"], in1.past(win, "pool", "biased", d))
                    dve.tensor_tensor(y1[:], zb[1][win.parity(d)][:, 2 * TOK:3 * TOK],
                                      y0b[win.parity(d)][:], ALU.add).then_inc(in2.sem["dve"], 1)
                if k == BASE_P1 + 4:
                    dve.wait_ge(in2.sem["dve"], in2.past(win, "dve", "y", d))
                    dve.bn_stats(st["y1"][:], y1[:]).then_inc(in2.sem["dve"], 1)
                if k == BASE_P1 + 5:
                    dve.wait_ge(in2.sem["dve"], win.apart(in2.past(win, "dve", "stats_y", d)))
                    dve.bn_aggr(mv["y1"][:], st["y1"][:]).then_inc(in2.sem["dve"], 1)
                if k == BASE_P1 + 10:
                    dve.wait_ge(in2.sem["pool"], in2.past(win, "pool", "rstd_y", d))
                    normalise(xn[1], y1, "y1").then_inc(in2.sem["dve"], 1)

            def join_x(win, k, d):
                if k == BASE_P2 + 2:
                    dve.wait_ge(join.sem["pe"], join.past(win, "pe", "read_out", d))
                    dve.wait_ge(in2.sem["pool"], in2.past(win, "pool", "biased", d))
                    dve.tensor_tensor(y2[:], zb[1][win.parity(d)][:, 2 * TOK:3 * TOK],
                                      y1b[win.parity(d)][:], ALU.add).then_inc(join.sem["dve"], 1)
                if k == BASE_P2 + 3:
                    dve.wait_ge(join.sem["dve"], join.past(win, "dve", "y", d))
                    dve.wait_ge(in1.sem["pool"], in1.past(win, "pool", "saved", d))
                    dve.tensor_tensor(x2[win.parity(d)][:], y2[:], x1[win.parity(d)][:], ALU.add).then_inc(join.sem["dve"], 1)

            def ffn_input(win, h, k, base, d):
                stg, r, name = ffn_in[h], rt[h], "f" + h
                src = (x0 if h == "a" else x2)[win.parity(d)]
                if k == base:
                    if h == "a":
                        dve.wait_ge(x_loaded, win.count(32, d, 32))
                    else:
                        dve.wait_ge(join.sem["dve"], join.past(win, "dve", "x", d))
                    dve.bn_stats(st[name][:], src[:]).then_inc(stg.sem["dve"], 1)
                if k == base + 1:
                    dve.wait_ge(stg.sem["dve"], win.apart(stg.past(win, "dve", "stats", d)))
                    dve.bn_aggr(mv[name][:], st[name][:]).then_inc(stg.sem["dve"], 1)
                if k == base + 8:
                    dve.wait_ge(stg.sem["pool"], stg.past(win, "pool", "rstd", d))
                    normalise(fn[h], src, name).then_inc(stg.sem["dve"], 1)
                if k == base + 15:
                    dve.wait_ge(stg.sem["act"], stg.past(win, "act", "full", d))
                    dve.scalar_tensor_tensor(
                        out=xs[win.parity(1)][:, 1, cols[h]], in0=fT[h][:], scalar=X_SCALE,
                        in1=xs[win.parity(1)][:, 0, cols[h]], op0=ALU.mult, op1=ALU.subtract).then_inc(stg.sem["dve"], 1)
                if k == base + 18:
                    dve.wait_ge(stg.sem["act"], win.apart(stg.past(win, "act", "logits_copied", d)))
                    dve.max(r["top"][:], r["logits"][:]).then_inc(stg.sem["dve"], 1)
                if k == base + 25:
                    dve.wait_ge(stg.sem["pool"], stg.past(win, "pool", "exps", d))
                    dve.tensor_reduce(r["total"][:], r["exps"][:], AX.X, ALU.add).then_inc(stg.sem["dve"], 1)
                if k == base + 26:
                    dve.wait_ge(stg.sem["dve"], stg.past(win, "dve", "total", d))
                    dve.reciprocal(r["inv"][:], r["total"][:]).then_inc(stg.sem["dve"], 1)
                if k == base + 28:
                    dve.wait_ge(stg.sem["pool"], win.apart(stg.past(win, "pool", "probs", d)))
                    dve.max(r["ptop"][:], r["probs"][:]).then_inc(stg.sem["dve"], 1)
                if k == base + 29:
                    dve.wait_ge(stg.sem["dve"], win.apart(stg.past(win, "dve", "top_probs", d)))
                    dve.max_index(r["index"][:], r["ptop"][:], r["probs"][:]).then_inc(stg.sem["dve"], 1)
                if k == base + 32:
                    dve.wait_ge(stg.sem["pool"], stg.past(win, "pool", "guarded", d))
                    dve.reciprocal(r["ipair"][:], r["guarded"][:]).then_inc(stg.sem["dve"], 1)

            def split_low(e):
                for g in range(2):
                    dve.wait_ge(hi_made, 2 * e + g + 1)
                    part = slice(e * F, (e + 1) * F)
                    dve.scalar_tensor_tensor(out=w_lo[g][:, part], in0=w32[g][:, part],
                                             scalar=W_SCALE, in1=w_hi[g][:, part], op0=ALU.mult,
                                             op1=ALU.subtract).then_inc(lo_made, 1)

            def multiply(win, h, w, j):
                n, c = CH[j % CHUNKS], cols[h]
                if h == halves(win, w)[0][0]:
                    dve.wait_ge(silu_ready, win.count(JOBS, w + 1, j + 1))
                dve.scalar_tensor_tensor(out=hidden[win.parity(w + j)][0:n, c], in0=gu[win.parity(w + j)][0:n, 1, c],
                                         scalar=UNSCALE, in1=silu[win.parity(w + j)][0:n, c], op0=ALU.mult,
                                         op1=ALU.mult).then_inc(hid_ready[h], 1)

            def window(win):
                for k in range(HALVES):
                    l = k % 2
                    for e in splits_at(win, k, LEAD_LO):
                        split_low(e)
                    if win.static == -1 and k == HALVES - 20:
                        biases()
                    at = rnn_step(win, l, k // 2)
                    if at:
                        d, t = at
                        q = win.parity(d)
                        pd, pt = (d, t - 1) if t else (d - 1, STEPS - 1)
                        dve.wait_ge(c_ready[l], win.count(STEPS, d, t + 1, l))
                        if t == 0:
                            dve.wait_ge((in1, in2)[l].sem["pool"], (in1, in2)[l].past(win, "pool", "gate", d))
                        dve.tensor_tensor_scan(
                            out=at_step(hist[l][q], t)[:, 0:8],
                            data0=at_step(gates[l][q], t)[:, 0:8],
                            data1=at_step(hist[l][win.parity(pd)], pt)[:, 2:10],
                            initial=0.0, op0=ALU.mult, op1=ALU.subtract).then_inc(h_ready[l], 1)
                    for h in "ab":
                        for j, w, on in jobs_at(win, k, MULTIPLY[h]):
                            for hh, d in on:
                                if hh == h:
                                    multiply(win, h, w, j)
                    if win.active(0, TILES):
                        in_1(win, k, 0)
                    if win.active(-1, TILES):
                        in_2(win, k, -1)
                    if win.active(-2, TILES):
                        join_x(win, k, -2)
                        ffn_input(win, "b", k, BASE_FB, -2)
                    if win.active(2, TILES):
                        ffn_input(win, "a", k, BASE_FA, 2)

            windows(dve, window)

        @block.tensor
        def _(pe):
            pe.wait_ge(consts_pool, 5)

            def project(win, stg, l, k, base, d):
                bank = zb[l][win.parity(d)]
                if k == base:
                    if l == 0 and win.active(d + 1, TILES):
                        pe.wait_ge(ffn_in["a"].sem["act"], ffn_in["a"].past(win, "act", "logits_copied", d + 1))
                    pe.wait_ge(stg.sem["dve"], stg.past(win, "dve", "normed", d))
                    pe.transpose(bank[:, 3 * TOK:4 * TOK], xn[l][:], ident[:]).then_inc(stg.sem["pe"], 1)
                if k == base + 3:
                    pe.wait_ge(stg.sem["act"], stg.past(win, "act", "affine", d))
                    pe.matmul(bank[:, 0:TOK], wi[:, l, P:2 * P], xaT[l][:], start=True, stop=False,
                              skip_group_check=True)
                if k == base + 4:
                    pe.matmul(bank[:, 0:TOK], bv_row[:, l, :], ones[:], start=False, stop=False,
                              skip_group_check=True)
                if k == base + 5:
                    pe.matmul(bank[:, TOK:2 * TOK], wi[:, l, 0:P], xaT[l][:], start=False, stop=True,
                                  skip_group_check=True).then_inc(stg.sem["pe"], 1)

            def read_out(win, stg, l, k, base, d):
                if k == base:
                    q = win.parity(d)
                    if l == 0:
                        pe.wait_ge(ffn_in["b"].sem["act"], ffn_in["b"].past(win, "act", "logits_copied", d - 2))
                    pe.wait_ge(h_ready[l], win.count(STEPS, d, STEPS, l))
                    pe.matmul(zb[1][q][:, 2 * TOK:3 * TOK], hist[l][q][:, :, 2], wo[:, l, :], start=True, stop=True,
                                  skip_group_check=True).then_inc(stg.sem["pe"], 1)

            def ffn_input(win, h, k, base, d, bank):
                stg = ffn_in[h]
                if k == base + 10:
                    pe.wait_ge(stg.sem["dve"], stg.past(win, "dve", "normed", d))
                    pe.transpose(bank[:, 3 * TOK:4 * TOK], fn[h][:], ident[:]).then_inc(stg.sem["pe"], 1)
                if k == base + 15:
                    pe.wait_ge(stg.sem["act"], stg.past(win, "act", "full", d))
                    if win.static == FIRST:
                        pe.wait_ge(gw_loaded, 16)
                    pe.matmul(bank[:, 2 * TOK:2 * TOK + EXPERTS], fT[h][:], gw[:], start=True,
                                  stop=True, skip_group_check=True).then_inc(stg.sem["pe"], 1)

            def last_of(win, w, early):
                pairs = (("a", w + 1), ("b", w - 3))
                if win.static is None:
                    return pairs[1:]
                return [(h, d) for h, d in pairs
                        if win.active(d, TILES) or (early and win.static + d == TILES)]

            def gate_or_up(win, on, w, j, g, passes):
                e, ch = divmod(j, CHUNKS)
                n, q = CH[ch], win.parity(w + j)
                c = slice(0, 2 * TOK) if wide(win, w, e) else span(on)
                src = xs[win.parity(w)]
                if g == 0 and 0 in passes:
                    for h, d in last_of(win, w, j < 2):
                        pe.wait_ge(hid_ready[h], win.count(JOBS, d, j - 1))
                    if j == 0:
                        for h, d in on:
                            pe.wait_ge(ffn_in[h].sem["dve"], ffn_in[h].past(win, "dve", "low", d))
                if win.static is not None and win.static + w == -1 and 0 in passes:
                    pe.wait_ge(lo_made, 2 * e + 2)
                dst = gu[q][0:n, g, c]
                r = rows[j]
                products = ((w_hi, 0), (w_hi, 1), (w_lo, 0), (w_lo, 1))
                last = 3 if g == 0 and wide(win, w, e) else 2
                passes = [p for p in passes if p <= last]
                for p in passes:
                    part, low = products[p]
                    mm = pe.matmul(dst, part[g][:, r], src[:, low, c], start=(g == 0 and p == 0),
                                   stop=(p == last), skip_group_check=True)
                if g == 1 and last in passes:
                    mm.then_inc(gu_ready, 1)

            def down(win, on, w, j, h):
                e, ch = divmod(j, CHUNKS)
                n = CH[ch]
                first, last = ("a", "b") if wide(win, w, e) else (on[0][0], on[-1][0])
                if not first <= h <= last:
                    return
                if h == first and ch == 0:
                    for m, (a, b) in enumerate(D_PARTS):
                        if win.static is not None and win.static + w == -1 and e == a:
                            pe.wait_ge(d_loaded[m], 16 * (2 if m == 0 else CHUNKS))
                    for hh, d in last_of(win, w, e < 2):
                        pe.wait_ge(weighted_ready[hh], win.count(FFNS, d, e - 1))
                for hh, d in on:
                    if hh == h:
                        pe.wait_ge(hid_ready[h], win.count(JOBS, d, j + 1))
                mm = pe.matmul(dn[win.parity(w + e)][:, cols[h]], hidden[win.parity(w + j)][0:n, cols[h]],
                               wd[0:n, j, :], start=(ch == 0 and h == first),
                               stop=(ch == CHUNKS - 1), skip_group_check=True)
                if ch == CHUNKS - 1 and h == last:
                    mm.then_inc(dn_ready, 1)

            def window(win):
                for k in range(HALVES):
                    l = k % 2
                    if win.static == -1 and k == HALVES - 20:
                        pe.wait_ge(w_loaded, 16 * 10)
                        pe.wait_ge(consts_dve, 4)
                        pe.wait_ge(consts_pool, POOL_CONSTS)
                    at = rnn_step(win, l, k // 2)
                    if at:
                        d, t = at
                        pd, pt = (d, t - 1) if t else (d - 1, STEPS - 1)
                        if t == 0:
                            pe.wait_ge((in1, in2)[l].sem["act"], (in1, in2)[l].past(win, "act", "gate_tanh", d))
                        pe.wait_ge(h_ready[l], win.count(STEPS, d, t, l))
                        z = zb[l][win.parity(d)][:, SEQS * t:SEQS * (t + 1)]
                        pe.matmul(z, wh[:, l, :], hist[l][win.parity(pd)][:, SEQS * pt:SEQS * (pt + 1), 2], start=False,
                                  stop=True, skip_group_check=True).then_inc(z_ready[l], 1)
                    for lag, g, passes in ((0, 0, (0,)), (1, 0, (1, 2, 3)), (2, 1, (0, 1)), (3, 1, (2,))):
                        for j, w, on in jobs_at(win, k, lag):
                            gate_or_up(win, on, w, j, g, passes)
                    for h in "ab":
                        for j, w, on in jobs_at(win, k, DOWN[h]):
                            down(win, on, w, j, h)
                    if win.active(0, TILES):
                        project(win, in1, 0, k, BASE_P0 + 15, 0)
                    if win.active(-1, TILES):
                        read_out(win, in2, 0, k, BASE_P1, -1)
                        project(win, in2, 1, k, BASE_P1 + 12, -1)
                    if win.active(-2, TILES):
                        read_out(win, join, 1, k, BASE_P2, -2)
                        ffn_input(win, "b", k, BASE_FB, -2, zb[1][win.parity(-2)])
                    if win.active(2, TILES):
                        ffn_input(win, "a", k, BASE_FA, 2, zb[0][win.parity(1)])

            windows(pe, window)


def kernel(**inputs):
    import numpy as np
    import concourse.bacc as bacc
    from concourse.bass_utils import run_bass_kernel_spmd

    a = {k: np.asarray(v) for k, v in inputs.items()}
    b_in = a["L0_attn_b_in"]
    D = b_in.shape[1] // 2

    def turned(w):
        return w.transpose(2, 0, 1).reshape(w.shape[2], -1)

    arrays = dict(
        x=a["L0_attn_x"],
        ln_g=a["L0_attn_ln_g"].T, ln_b=a["L0_attn_ln_b"].T,
        w_in=a["L0_attn_W_in"].transpose(0, 2, 1),
        b_gate=b_in[:, :D].T, b_cand=b_in[:, D:], b_h=a["L0_attn_b_h"],
        w_h=a["L0_attn_W_h"].transpose(0, 2, 1), w_out=a["L0_attn_W_out"].transpose(0, 2, 1),
        b_out=a["L0_attn_b_out"], gate_w=a["L0_ffn_gate_w"].T,
        expert_gate=turned(a["L0_ffn_expert_gate"]), expert_up=turned(a["L0_ffn_expert_up"]),
        expert_down=a["L0_ffn_expert_down"].transpose(0, 2, 1),
        shared_gate=a["L0_ffn_shared_gate"].T, shared_up=a["L0_ffn_shared_up"].T,
        shared_down=a["L0_ffn_shared_down"].T,
    )
    nc = bacc.Bacc("TRN2", target_bir_lowering=False, num_devices=1)
    args, maps = [], {}
    for name, v in arrays.items():
        maps[name] = np.ascontiguousarray(v)
        args.append(nc.dram_tensor(name, v.shape, mybir.dt.from_np(v.dtype), kind="ExternalInput").ap())
    args.append(nc.dram_tensor("out", a["L0_attn_x"].shape, F32, kind="ExternalOutput").ap())
    macaron(nc, *args)
    r = run_bass_kernel_spmd(nc, [maps], core_ids=[0])
    return r.results[0]["out"]
```
